# Optimizing a Trainium2 kernel written in Bass

```python
import numpy as np
import jax
import jax.numpy as jnp

def _softmax(x, axis=-1):
    return jax.nn.softmax(x, axis=axis)

def _gelu(x):
    return jax.nn.gelu(x, approximate=True)

def _silu(x):
    return jax.nn.silu(x)

def _sigmoid(x):
    return jax.nn.sigmoid(x)

def _layernorm(x, axis=-1, eps=1e-05):
    m = jnp.mean(x, axis=axis, keepdims=True)
    v = jnp.var(x, axis=axis, keepdims=True)
    return (x - m) / jnp.sqrt(v + eps)

def _scatter_add(tgt, idx, src, axis=0):
    return tgt.at[idx].add(src)

def _segment_sum(src, seg, n):
    return jax.ops.segment_sum(src, seg, n)
kernel_name = 'mk_gnn_resnorm_d1_gnn_r8_579c97'

def setup_inputs(seed: int=0):
    np.random.seed(seed)
    _w = jnp.asarray

    def _rec_inputs():
        import jax
        import jax.numpy as jnp
        _gk = jax.random.key(seed)
        x = -0.0001006 + 1 * jax.random.normal(jax.random.fold_in(_gk, 1), (6250, 96), jnp.float32)
        _s = jax.random.randint(jax.random.fold_in(_gk, 2), (50000,), 0, 6250, jnp.int32)
        _d = jax.random.randint(jax.random.fold_in(_gk, 3), (50000,), 0, 6250, jnp.int32)
        _loop = jnp.arange(6250, dtype=jnp.int32)
        src = jnp.concatenate([_s, _d, _loop])
        dst = jnp.concatenate([_d, _s, _loop])
        _o = jnp.argsort(dst, stable=True)
        src = src[_o]
        dst = dst[_o]
        return (x, src, dst)
    x, src, dst = _rec_inputs()

    def _L0_gnn_setup():
        import jax, jax.numpy as jnp
        import numpy as np
        N_NODES = 6250
        N_EDGES = 100000
        D_MODEL = 96
        HEADS = 4
        key = jax.random.key(seed)
        ks = jax.random.split(key, 6)
        scale = 1.0 / np.sqrt(D_MODEL)
        return {'embeds': jax.random.normal(ks[0], (N_NODES, D_MODEL), dtype=jnp.float32), 'qW': jax.random.normal(ks[1], (D_MODEL, D_MODEL), dtype=jnp.float32) * scale, 'kW': jax.random.normal(ks[2], (D_MODEL, D_MODEL), dtype=jnp.float32) * scale, 'vW': jax.random.normal(ks[3], (D_MODEL, D_MODEL), dtype=jnp.float32) * scale, 'rows': jax.random.randint(ks[4], (N_EDGES,), 0, N_NODES, dtype=jnp.int32), 'cols': jax.random.randint(ks[5], (N_EDGES,), 0, N_NODES, dtype=jnp.int32)}
    _L0_gnn_all = _L0_gnn_setup()
    _L0_gnn_in = {k: v for k, v in _L0_gnn_all.items() if k in ('qW', 'kW', 'vW')}
    del _L0_gnn_all
    return {'x': x, 'src': src, 'dst': dst, 'L0_gnn_qW': _L0_gnn_in['qW'], 'L0_gnn_kW': _L0_gnn_in['kW'], 'L0_gnn_vW': _L0_gnn_in['vW']}

def reference(x, src, dst, L0_gnn_qW, L0_gnn_kW, L0_gnn_vW):
    import jax
    import jax.numpy as jnp

    def _L0_gnn_ref(embeds, qW, kW, vW, rows, cols):
        import jax, jax.numpy as jnp
        import numpy as np
        N_NODES = 6250
        N_EDGES = 100000
        D_MODEL = 96
        HEADS = 4
        nvar, d = embeds.shape
        dh = d // HEADS
        e = rows.shape[0]
        q = (embeds[rows] @ qW).reshape(e, HEADS, dh)
        k = (embeds[cols] @ kW).reshape(e, HEADS, dh)
        v = (embeds[cols] @ vW).reshape(e, HEADS, dh)
        scores = jnp.clip(jnp.einsum('ehd,ehd->eh', q, k), -10.0, 10.0)
        exp_s = jnp.exp(scores)
        norms = jax.ops.segment_sum(exp_s, rows, num_segments=nvar)[rows]
        w = exp_s / (norms + 1e-08)
        res = jax.ops.segment_sum(w[:, :, None] * v, rows, num_segments=nvar).reshape(nvar, d)
        return embeds + res
    x = _layernorm(x + _L0_gnn_ref(x, L0_gnn_qW, L0_gnn_kW, L0_gnn_vW, src, dst), axis=-1)
    return x

_drawn_inputs = setup_inputs


def setup_inputs(seed=0):
    import zlib

    import numpy as np

    out = dict(_drawn_inputs(seed))
    spreads = {}
    factors = {}
    for name, (base, spread) in spreads.items():
        noise = np.random.default_rng([zlib.crc32(name.encode()), seed]).standard_normal(out[name].shape)
        drawn = base * np.exp(spread * noise) if base else spread * noise
        out[name] = jnp.asarray(drawn.astype(out[name].dtype))
    for name, factor in factors.items():
        out[name] = (out[name] * factor).astype(out[name].dtype)
    return out
```

```python
import concourse.bass as bass
from concourse import mybir
from contextlib import ExitStack



def gnn(nc, x, src, dst, qW, kW, vW, out):
    f32, i32 = mybir.dt.float32, mybir.dt.int32
    f16, bf16 = mybir.dt.float16, mybir.dt.bfloat16
    ALU = mybir.AluOpType
    ACT = mybir.ActivationFunctionType
    AX = mybir.AxisListType

    P = 128
    N, D = x.shape
    E = src.shape[0]
    HEADS = 4
    DH = D // HEADS
    NB = (N + P - 1) // P
    LASTB = N - (NB - 1) * P
    EP, EC = 125, E // 125
    assert EP * EC == E
    RW = D + HEADS
    U = 4
    RING = 4

    GC = [210, 213, 213, 214]
    assert sum(GC) == EC
    G = len(GC)
    GT = [-(-((EP * c + NB * (P - 1)) // P) // U) * U for c in GC]
    assert max(GT) + 1 <= 512
    C0 = [sum(GC[:g]) for g in range(G + 1)]
    B0 = [sum(GT[:g]) // U for g in range(G + 1)]
    NT = sum(GT)
    CMAX = max(GC)
    WCH = 54
    PC = 7
    NPC = NB // PC
    assert NPC * PC == NB
    WEAVE = [0] + [GC[g] // (B0[g] - B0[g - 1]) for g in range(1, G)]

    kv_dram = nc.dram_tensor("kv_table", [NB * P, 2 * D], f32).ap()

    with ExitStack() as ctx:
        def sb(name, shape, dt):
            return ctx.enter_context(nc.sbuf_tensor(name, shape, dt))

        def pb(name, shape, dt):
            return ctx.enter_context(nc.psum_tensor(name, shape, dt))

        def sem(name):
            return ctx.enter_context(nc.semaphore(name))

        iota_i = sb("iota_i", [P, 512], i32)
        iota_f = sb("iota_f", [P, 512], f32)
        iota1_bf = sb("iota1_bf", [P, P], bf16)
        iota0_h = sb("iota0_h", [P, P], f16)
        part_i = sb("part_i", [P, 1], i32)
        part_f = sb("part_f", [P, 1], f32)
        ident_f = sb("ident_f", [P, P], f32)
        ident_bf = sb("ident_bf", [P, P], bf16)
        tri_h = sb("tri_h", [P, P], f16)
        ones_h = sb("ones_h", [P, P], f16)
        w_all = sb("w_all", [D, 3 * D], f32)
        xc = sb("xc", [P, 2, PC, D], f32)
        xlast = sb("xlast", [P, D], f32)
        xT = sb("xT", [D, 2, P], f32)
        q3 = sb("q3", [P, 3, NB, D], bf16)
        kvs = sb("kvs", [P, PC, 2 * D], f32)
        acc = sb("acc", [P, NB * RW], f32)
        qf = acc[:, 0:NB * D].rearrange("p (b d) -> p b d", b=NB)
        acc_b = acc[:, :].rearrange("p (b d) -> p b d", b=NB)
        src_i = sb("src_i", [EP, EC], i32)
        dst_i = sb("dst_i", [EP, EC], i32)
        tmp_i = sb("tmp_i", [EP, EC], i32)
        bin_h = sb("bin_h", [EP, EC], f16)
        pay_a = sb("pay_a", [EP, EC], f32)
        pay_b = sb("pay_b", [EP, EC], f32)
        pos_f = sb("pos_f", [EP, EC], f32)
        pos_p = sb("pos_p", [EP, EC], f32)
        pos_t = sb("pos_t", [EP, EC], f32)
        inbin_m = sb("inbin_m", [EP, NB * CMAX], f16)
        rank_m = sb("rank_m", [EP, NB * CMAX], f16)
        rsel = sb("rsel", [EP, NB, WCH], f32)
        ends = sb("ends", [EP, NB], f16)
        cnt = sb("cnt", [EP, NB], f16)
        need_i = sb("need_i", [P, NB], i32)
        need = sb("need", [P, NB], f32)
        tend = sb("tend", [P, NB], f32)
        tdiag = sb("tdiag", [P, NB], f32)
        tend_p = sb("tend_p", [P, 1], f32)
        after = sb("after", [P, 512], f16)
        adj = sb("adj", [P, NB], f32)
        adj2 = sb("adj2", [P, NB], f32)
        lhs_a = sb("lhs_a", [EP, RING, P], f16)
        lhs_b = sb("lhs_b", [EP, RING, P], f16)
        theta = sb("theta", [EP, RING, 512], f16)
        cum_a = sb("cum_a", [P, 512], f32)
        cum_b = sb("cum_b", [P, 512], f32)
        dif_a = iota_i
        dif_b = sb("dif_b", [P, 512], i32)
        dst_s = sb("dst_s", [P, NT], i32)
        loc_i = sb("loc_i", [P, 512], i32)
        loc_s = sb("loc_s", [P, NT], f32)
        blk_s = sb("blk_s", [1, NT], i32)
        idx = sb("idx", [P, RING, U], i32)
        kv = sb("kv", [P, RING, U, 2 * D], f32)
        oneh = sb("oneh", [P, RING, U, P], bf16)
        oneh_f = sb("oneh_f", [P, RING, U, P], f32)
        onehT = sb("onehT", [P, 2, U * P], bf16)
        prod = sb("prod", [P, 2, U * D], f32)
        score = sb("score", [P, 2, U * HEADS], f32)
        clipped = sb("clipped", [P, 2, U * HEADS], f32)
        wv = sb("wv", [P, 2, U, RW], f32)
        den = sb("den", [P, NB, HEADS], f32)
        mean = sb("mean", [P, PC], f32)
        var = sb("var", [P, PC], f32)
        std = sb("std", [P, PC], f32)
        inv = sb("inv", [P, PC], f32)
        kv_m = kv[:, :, :, :].rearrange("p r u d -> p (r u d)")
        cent = kv_m[:, 0:PC * D].rearrange("p (b d) -> p b d", b=PC)
        sq = kv_m[:, PC * D:2 * PC * D].rearrange("p (b d) -> p b d", b=PC)
        yout = kvs[:, :, :].rearrange("p a b -> p (a b)").rearrange("p (i b d) -> p i b d", i=2, d=D)

        ps_a = pb("ps_a", [P, 512], f32)
        ps_b = pb("ps_b", [P, 512], f32)
        ps_t = [pb(f"ps_t{i}", [P, 1024], bf16) for i in range(2)]
        ps_q = [pb(f"ps_q{i}", [P, 512], f32) for i in range(2)]
        ps_r = [pb(f"ps_r{i}", [P, 512], f32) for i in range(2)]
        ps_m = ps_r[1]

        s_x = [sem("s_x0"), sem("s_x1")]
        s_xe = [sem("s_xe0"), sem("s_xe1")]
        s_xl = sem("s_xl")
        s_w = sem("s_w")
        s_src = sem("s_src")
        s_dst = sem("s_dst")
        s_iota = sem("s_iota")
        s_const = sem("s_const")
        s_xpad = sem("s_xpad")
        s_xt = sem("s_xt")
        s_xtc = sem("s_xtc")
        s_prj = sem("s_prj")
        s_prjc = sem("s_prjc")
        s_kvst = sem("s_kvst")
        s_split = sem("s_split")
        s_rest = sem("s_rest")
        s_own = sem("s_own")
        s_cnt = sem("s_cnt")
        s_pre = sem("s_pre")
        s_after = sem("s_after")
        s_tab = sem("s_tab")
        s_blk = sem("s_blk")
        s_pos = sem("s_pos")
        s_lhs = sem("s_lhs")
        s_theta = sem("s_theta")
        s_bin = sem("s_bin")
        s_cum = sem("s_cum")
        s_sorted = sem("s_sorted")
        s_acc0 = sem("s_acc0")
        s_idx = sem("s_idx")
        s_kv = [sem(f"s_kv{i}") for i in range(RING)]
        s_oneh = sem("s_oneh")
        s_ot = sem("s_ot")
        s_otc = sem("s_otc")
        s_of = sem("s_of")
        s_q = sem("s_q")
        s_prod = sem("s_prod")
        s_score = sem("s_score")
        s_clip = sem("s_clip")
        s_exp = sem("s_exp")
        s_wv = sem("s_wv")
        s_res = sem("s_res")
        s_acc = sem("s_acc")
        s_cent = sem("s_cent")
        s_sq = sem("s_sq")
        s_var = sem("s_var")
        s_std = sem("s_std")
        s_y = sem("s_y")
        s_out = [sem("s_out0"), sem("s_out1")]
        s_past = sem("s_past")

        def known_zero(v):
            return isinstance(v, int) and v <= 0

        def wait(eng, s, v):
            if not known_zero(v):
                eng.wait_ge(s, v)

        def batches(eng, g, body):
            lo, hi = B0[g], B0[g + 1]
            a = lo + 4
            b = a + (hi - 3 - a) // 4 * 4
            for m in range(lo - 3, a):
                body(m, m % 4)
            with eng.Fori(a, b - 3, 4) as i:
                for k in range(4):
                    body(i + k, (a + k) % 4)
            for m in range(b, hi + 2):
                body(m, m % 4)

        def inside(n, g):
            return not isinstance(n, int) or B0[g] <= n < B0[g + 1]

        def woven(g, m, mm, step):
            if g + 1 < G and inside(m, g):
                k = WEAVE[g + 1]
                for j in range(k):
                    c = (m - B0[g]) * k + C0[g + 1] + j
                    step(g + 1, c, ((mm - B0[g]) * k + C0[g + 1] + j) % RING)

        def rest_of_sorting(eng, g, step):
            lo = C0[g] + (WEAVE[g] * (B0[g] - B0[g - 1]) if g else 0)
            hi = C0[g + 1]
            a = min(lo + RING, hi)
            b = a + max(0, hi - 1 - a) // RING * RING
            for c in range(lo, a):
                step(g, c, c % RING)
            if b > a:
                with eng.Fori(a, b - RING + 1, RING) as i:
                    for k in range(RING):
                        step(g, i + k, (a + k) % RING)
            for c in range(b, hi):
                step(g, c, c % RING)

        block = ctx.enter_context(nc.Block())

        @block.sync
        def _(sp):
            sp.dma_start(src_i[:, :], src.rearrange("(p c) -> p c", c=EC)).then_inc(s_src, 16)
            sp.dma_start(dst_i[:, :], dst.rearrange("(p c) -> p c", c=EC)).then_inc(s_dst, 16)

            def load_x(i, slot_sem):
                n = PC if i < NPC - 1 else PC - 1
                sp.dma_start(xc[:, i % 2, 0:n, :],
                             x[i * PC * P:(i * PC + n) * P, :].rearrange("(b p) d -> p b d", p=P)).then_inc(slot_sem[i % 2], 16)

            for i, w in enumerate((qW, kW, vW)):
                sp.dma_start(w_all[:, i * D:(i + 1) * D], w).then_inc(s_w, 16)
            sp.wait_ge(s_xpad, 1)
            sp.dma_start(xlast[0:LASTB, :], x[(NB - 1) * P:N, :]).then_inc(s_xl, 16)
            load_x(0, s_x)
            load_x(1, s_x)
            kv_rows = kv_dram.rearrange("(i b p) d -> i p b d", p=P, b=PC)
            for i in range(NPC):
                sp.wait_ge(s_prjc, PC * (i + 1))
                sp.dma_start(kv_rows[i], kvs[:, :, :]).then_inc(s_kvst, 16)
                if i + 2 < NPC:
                    load_x(i + 2, s_x)
            load_x(0, s_xe)
            load_x(1, s_xe)
            for i in range(NPC):
                sp.wait_ge(s_y, i + 1)
                if i < NPC - 1:
                    sp.dma_start(out[i * PC * P:(i + 1) * PC * P, :].rearrange("(b p) d -> p b d", p=P),
                                 yout[:, i % 2, :, :]).then_inc(s_out[i % 2], 16)
                else:
                    sp.dma_start(out[i * PC * P:(NB - 1) * P, :].rearrange("(b p) d -> p b d", p=P),
                                 yout[:, i % 2, 0:PC - 1, :]).then_inc(s_out[i % 2], 16)
                    sp.dma_start(out[(NB - 1) * P:N, :], yout[0:LASTB, i % 2, PC - 1, :]).then_inc(s_out[i % 2], 16)
                if i + 2 < NPC:
                    load_x(i + 2, s_xe)
            last = (NPC - 1) % 2
            sp.wait_ge(s_out[last], 16 * ((NPC + 1) // 2 + 1))
            sp.wait_ge(s_out[1 - last], 16 * (NPC // 2))

        @block.gpsimd
        def _(pool):
            nc.gpsimd.memset(xlast[:, :], 0.0).then_inc(s_xpad, 1)
            nc.gpsimd.iota(iota_i[:, :], [[1, 512]], base=0, channel_multiplier=0).then_inc(s_iota, 1)
            nc.gpsimd.iota(part_i[:, :], [[1, 1]], base=0, channel_multiplier=1).then_inc(s_iota, 1)
            nc.gpsimd.memset(ones_h[:, :], 1.0).then_inc(s_iota, 1)
            pool.wait_ge(s_split, 1)
            nc.gpsimd.tensor_tensor(qf, qf, q3[:, 0, :, :], ALU.subtract).then_inc(s_rest, 1)
            pool.wait_ge(s_split, 2)
            nc.gpsimd.tensor_tensor(q3[:, 2, :, :], qf, q3[:, 1, :, :], ALU.subtract).then_inc(s_rest, 1)
            pool.wait_ge(s_rest, 2)
            nc.gpsimd.memset(acc[:, :], 0.0).then_inc(s_acc0, 1)
            pool.wait_ge(s_kvst, 16 * NPC)

            def gathers(n, nm):
                pool.wait_ge(s_idx, n + 1)
                pool.sem_inc(s_past, 1)
                for u in range(U):
                    nc.gpsimd.indirect_dma_start(
                        kv[:, nm, u, :], None, kv_dram,
                        bass.IndirectOffsetOnAxis(ap=idx[:, nm, u:u + 1], axis=0)).then_inc(s_kv[nm], 16)

            for g in range(G):
                batches(pool, g, lambda m, mm: gathers(m + 3, (mm + 3) % RING) if inside(m + 3, g) else None)

        @block.tensor
        def _(pe):
            pe.wait_ge(s_w, 48)
            pe.wait_ge(s_const, 1)
            for b in range(NB):
                i, j = b // PC, b % PC
                if j == 0:
                    pe.wait_ge(s_x[i % 2], 16 * (i // 2 + 1))
                if b == NB - 1:
                    pe.wait_ge(s_xl, 16)
                if b >= 2:
                    pe.wait_ge(s_xtc, b - 1)
                nc.tensor.transpose(ps_q[b % 2][0:D, 0:P], xc[:, i % 2, j, :] if b < NB - 1 else xlast[:, :], ident_f[:, :]).then_inc(s_xt, 1)
                pe.wait_ge(s_xtc, b + 1)
                if b >= 2:
                    pe.wait_ge(s_prjc, b - 1)
                nc.tensor.matmul(ps_r[b % 2][:, 0:3 * D], xT[:, b % 2, :], w_all[:, :],
                                 start=True, stop=True).then_inc(s_prj, 1)

            def ranks(g):
                pe.wait_ge(s_cnt, g + 1)
                nc.tensor.matmul(ps_m[:, 0:NB], tri_h[0:EP, :], cnt[:, :], start=True, stop=True)
                nc.tensor.matmul(ps_m[:, 64:64 + NB], ones_h[0:EP, :], cnt[:, :],
                                 start=True, stop=True).then_inc(s_pre, 1)
                pe.wait_ge(s_after, g + 1)
                nc.tensor.matmul(ps_m[:, 0:GT[g]], ones_h[:, :], after[:, 0:GT[g]],
                                 start=True, stop=True).then_inc(s_tab, 1)

            def step(g, c, cm):
                first, last = isinstance(c, int) and c == C0[g], isinstance(c, int) and c == C0[g + 1] - 1
                if first and g:
                    pe.wait_ge(s_cum, g)
                pe.wait_ge(s_lhs, c + 1)
                pe.wait_ge(s_theta, c + 1)
                w = GT[g] + 1
                nc.tensor.matmul(ps_a[:, 0:w], lhs_a[:, cm, :], theta[:, cm, 0:w], start=first, stop=last)
                nc.tensor.matmul(ps_b[:, 0:w], lhs_b[:, cm, :], theta[:, cm, 0:w],
                                 start=first, stop=last).then_inc(s_bin, 1)

            def tiles(g, m, mm):
                n, nm = m + 2, (mm + 2) % 4
                if inside(n, g):
                    pe.wait_ge(s_oneh, n + 1)
                    wait(pe, s_otc, n - 1)
                    for u in range(U):
                        last = nc.tensor.transpose(ps_t[nm % 2][:, u * P:(u + 1) * P], oneh[:, nm, u, :], ident_bf[:, :])
                    last.then_inc(s_ot, 1)
                n, nm = m + 1, (mm + 1) % 4
                if inside(n, g):
                    blks = nc.values_load_multi_w_load_instructions(
                        blk_s[0:1, bass.ds(n * U, U)], engines=[mybir.EngineType.PE], min_val=0, max_val=NB - 1,
                        skip_runtime_bounds_check_because="clamped when the table is made")[1]
                    pe.wait_ge(s_otc, n + 1)
                    wait(pe, s_prod, n - 1)
                    for u in range(U):
                        for i in range(3):
                            last = nc.tensor.matmul(ps_q[nm % 2][:, u * D:(u + 1) * D],
                                                    onehT[:, nm % 2, u * P:(u + 1) * P],
                                                    q3[:, i, bass.ds(blks[u], 1), :].rearrange("p a d -> p (a d)"),
                                                    start=(i == 0), stop=(i == 2))
                    last.then_inc(s_q, 1)
                n, nm = m - 1, (mm - 1) % 4
                if inside(n, g):
                    pe.wait_ge(s_of, n + 1)
                    pe.wait_ge(s_wv, n + 1)
                    wait(pe, s_acc, U * (n - 1))
                    for u in range(U):
                        last = nc.tensor.matmul(ps_r[nm % 2][:, u * RW:(u + 1) * RW], oneh_f[:, nm, u, :],
                                                wv[:, nm % 2, u, :], start=True, stop=True)
                    last.then_inc(s_res, 1)
                woven(g, m, mm, step)

            ranks(0)
            rest_of_sorting(pe, 0, step)
            pe.wait_ge(s_rest, 2)
            for g in range(G):
                if g + 1 < G:
                    ranks(g + 1)
                pe.wait_ge(s_blk, g + 1)
                batches(pe, g, lambda m, mm: tiles(g, m, mm))
                if g + 1 < G:
                    rest_of_sorting(pe, g + 1, step)

        @block.scalar
        def _(act):
            for b in range(NB):
                j = b % PC
                act.wait_ge(s_xt, b + 1)
                if b >= 2:
                    act.wait_ge(s_prj, b - 1)
                nc.scalar.activation(xT[:, b % 2, :], ps_q[b % 2][0:D, 0:P], ACT.Copy).then_inc(s_xtc, 1)
                act.wait_ge(s_prj, b + 1)
                nc.scalar.activation(qf[:, b, :], ps_r[b % 2][:, 0:D], ACT.Copy)
                if j == 0 and b:
                    act.wait_ge(s_kvst, 16 * (b // PC))
                nc.scalar.activation(kvs[:, j, :], ps_r[b % 2][:, D:3 * D], ACT.Copy).then_inc(s_prjc, 1)
            act.wait_ge(s_prjc, NB)
            nc.scalar.activation(q3[:, 0, :, :], qf, ACT.Copy).then_inc(s_split, 1)
            act.wait_ge(s_rest, 1)
            nc.scalar.activation(q3[:, 1, :, :], qf, ACT.Copy).then_inc(s_split, 1)

            def step(g, c, cm):
                wait(act, s_bin, c - RING + 1)
                act.sem_inc(s_past, 1)
                w = GT[g] + 1
                nc.scalar.activation(theta[:, cm, 0:w], iota_f[0:EP, 0:w], ACT.Sign,
                                     bias=pos_t[:, bass.ds(c, 1)]).then_inc(s_theta, 1)

            def tiles(g, m, mm):
                n, nm = m + 2, (mm + 2) % 4
                if inside(n, g):
                    wait(act, s_q, n - 1)
                    act.wait_ge(s_ot, n + 1)
                    nc.scalar.activation(onehT[:, nm % 2, :], ps_t[nm % 2][:, 0:U * P], ACT.Copy).then_inc(s_otc, 1)
                    wait(act, s_res, n - RING + 1)
                    nc.scalar.activation(oneh_f[:, nm, :, :], oneh[:, nm, :, :], ACT.Copy).then_inc(s_of, 1)
                n, nm = m, mm
                if inside(n, g):
                    wait(act, s_res, n - 1)
                    act.wait_ge(s_clip, n + 1)
                    nc.scalar.activation(wv[:, nm % 2, :, D:RW],
                                         clipped[:, nm % 2, :].rearrange("p (u h) -> p u h", h=HEADS),
                                         ACT.Exp).then_inc(s_exp, 1)
                n, nm = m + 3, (mm + 3) % 4
                if inside(n, g):
                    wait(act, s_wv, n - RING + 1)
                    act.sem_inc(s_past, 1)
                    nc.scalar.activation(idx[:, nm, :], dst_s[:, bass.ds(n * U, U)], ACT.Copy).then_inc(s_idx, 1)
                woven(g, m, mm, step)

            def read_sorted(g):
                act.wait_ge(s_bin, C0[g + 1])
                if g:
                    act.wait_ge(s_sorted, g)
                w = GT[g] + 1
                nc.scalar.activation(cum_a[:, 0:w], ps_a[:, 0:w], ACT.Copy)
                nc.scalar.activation(cum_b[:, 0:w], ps_b[:, 0:w], ACT.Copy).then_inc(s_cum, 1)

            act.wait_ge(s_pos, 1)
            rest_of_sorting(act, 0, step)
            read_sorted(0)
            for g in range(G):
                if g + 1 < G:
                    act.wait_ge(s_pos, g + 2)
                act.wait_ge(s_sorted, g + 1)
                batches(act, g, lambda m, mm: tiles(g, m, mm))
                if g + 1 < G:
                    rest_of_sorting(act, g + 1, step)
                    read_sorted(g + 1)
            for i in range(NPC):
                act.wait_ge(s_cent, i + 1)
                nc.scalar.activation(sq[:, :, :], cent[:, :, :], ACT.Square).then_inc(s_sq, 1)
                act.wait_ge(s_var, i + 1)
                nc.scalar.activation(std[:, :], var[:, :], ACT.Sqrt).then_inc(s_std, 1)

        @block.vector
        def _(dve):
            own = [0]

            def link(ins):
                own[0] += 1
                ins.then_inc(s_own, 1)
                dve.wait_ge(s_own, own[0])

            dve.wait_ge(s_iota, 3)
            nc.vector.tensor_copy(iota_f[:, :], iota_i[:, :])
            link(nc.vector.tensor_copy(part_f[:, :], part_i[:, :]))
            nc.vector.tensor_scalar(ident_f[:, :], iota_f[:, 0:P], part_f[:, 0:1], None, ALU.is_equal)
            nc.vector.tensor_scalar(ident_bf[:, :], iota_f[:, 0:P], part_f[:, 0:1], None, ALU.is_equal)
            nc.vector.tensor_scalar(tri_h[:, :], iota_f[:, 0:P], part_f[:, 0:1], None, ALU.is_gt)
            nc.vector.tensor_scalar(iota1_bf[:, :], iota_f[:, 0:P], 1.0, None, ALU.add)
            link(nc.vector.tensor_copy(iota0_h[:, :], iota_f[:, 0:P]))
            nc.vector.memset(after[:, 0:1], 0.0).then_inc(s_const, 1)
            dve.wait_ge(s_src, 16)
            link(nc.vector.tensor_scalar(tmp_i[:, :], src_i[:, :], 7, None, ALU.logical_shift_right))
            link(nc.vector.tensor_copy(bin_h[:, :], tmp_i[:, :]))
            link(nc.vector.tensor_scalar(src_i[:, :], src_i[:, :], P - 1, 3, ALU.bitwise_and, ALU.logical_shift_left))
            dve.wait_ge(s_dst, 16)
            link(nc.vector.tensor_scalar(tmp_i[:, :], dst_i[:, :], 10, None, ALU.logical_shift_right))
            link(nc.vector.scalar_tensor_tensor(pay_a[:, :], src_i[:, :], 8.0, tmp_i[:, :], ALU.add, ALU.add))
            link(nc.vector.tensor_scalar(tmp_i[:, :], dst_i[:, :], 1023, None, ALU.bitwise_and))
            link(nc.vector.tensor_copy(pay_b[:, :], tmp_i[:, :]))

            def ranks(g):
                c0, c1, C = C0[g], C0[g + 1], GC[g]
                inbin = inbin_m[:, 0:NB * C].rearrange("p (b c) -> p b c", b=NB)
                rank = rank_m[:, 0:NB * C].rearrange("p (b c) -> p b c", b=NB)
                link(nc.vector.tensor_tensor(inbin,
                                             bin_h[:, c0:c1].unsqueeze(1).to_broadcast([EP, NB, C]),
                                             iota0_h[0:EP, 0:NB].unsqueeze(2).to_broadcast([EP, NB, C]),
                                             ALU.is_equal))
                link(nc.vector.tensor_tensor_scan(rank_m[:, 0:NB * C], inbin_m[:, 0:NB * C], inbin_m[:, 0:NB * C],
                                                  0.0, ALU.add, ALU.max))
                link(nc.vector.tensor_copy(ends[:, :], rank[:, :, C - 1]))
                nc.vector.tensor_copy(cnt[:, 0:1], ends[:, 0:1])
                nc.vector.tensor_tensor(cnt[:, 1:NB], ends[:, 1:NB], ends[:, 0:NB - 1], ALU.subtract).then_inc(s_cnt, 1)
                dve.wait_ge(s_pre, g + 1)
                link(nc.vector.tensor_scalar(need_i[:, :], ps_m[:, 64:64 + NB], float(P - 1), None, ALU.add))
                link(nc.vector.tensor_scalar(need_i[:, :], need_i[:, :], 7, None, ALU.logical_shift_right))
                link(nc.vector.tensor_copy(need[:, :], need_i[:, :]))
                link(nc.vector.tensor_tensor_scan(tend[:, :], need[:, :], need[:, :], 0.0, ALU.add, ALU.max))
                link(nc.vector.tensor_tensor(adj[:, :], tend[:, :], need[:, :], ALU.subtract))
                link(nc.vector.scalar_tensor_tensor(adj2[:, :], adj[:, :], float(P), ps_m[:, 0:NB], ALU.mult, ALU.add))
                link(nc.vector.tensor_tensor(adj[0:EP, :], adj2[0:EP, :], ends[:, :], ALU.subtract))
                link(nc.vector.scalar_tensor_tensor(adj2[0:EP, :], adj[0:EP, :], -1.0, cnt[:, :], ALU.add, ALU.add))
                link(nc.vector.tensor_tensor(tdiag[:, :], tend[:, :], ident_f[:, 0:NB], ALU.mult))
                link(nc.vector.tensor_reduce(tend_p[:, :], tdiag[:, :], axis=AX.X, op=ALU.add))
                nc.vector.tensor_scalar(after[:, 0:GT[g]], iota_f[:, 0:GT[g]], tend_p[:, 0:1], None,
                                        ALU.is_ge).then_inc(s_after, 1)
                for w0 in range(0, C, WCH):
                    w = min(WCH, C - w0)
                    link(nc.vector.tensor_tensor(rsel[:, :, 0:w], rank[:, :, w0:w0 + w],
                                                 adj2[0:EP, :].unsqueeze(2).to_broadcast([EP, NB, w]), ALU.add))
                    link(nc.vector.tensor_tensor(rsel[:, :, 0:w], rsel[:, :, 0:w], inbin[:, :, w0:w0 + w], ALU.mult))
                    link(nc.vector.tensor_reduce(pos_f[:, c0 + w0:c0 + w0 + w],
                                                 rsel[:, :, 0:w].rearrange("p b c -> p c b"), axis=AX.X, op=ALU.add))
                link(nc.vector.tensor_copy(tmp_i[:, c0:c1], pos_f[:, c0:c1]))
                link(nc.vector.tensor_scalar(src_i[:, c0:c1], tmp_i[:, c0:c1], P - 1, None, ALU.bitwise_and))
                link(nc.vector.tensor_copy(pos_p[:, c0:c1], src_i[:, c0:c1]))
                link(nc.vector.tensor_scalar(tmp_i[:, c0:c1], tmp_i[:, c0:c1], 7, None, ALU.logical_shift_right))
                link(nc.vector.tensor_scalar(pos_t[:, c0:c1], tmp_i[:, c0:c1], -1.0, -0.5, ALU.mult, ALU.add))
                nc.vector.tensor_copy(pos_f[:, c0:c0 + 1], pos_p[:, c0:c0 + 1]).then_inc(s_pos, 1)
                dve.wait_ge(s_tab, g + 1)
                t0 = B0[g] * U
                nc.vector.tensor_scalar(blk_s[0:1, t0:t0 + GT[g]], ps_m[0:1, 0:GT[g]], float(NB - P), float(NB - 1),
                                        ALU.add, ALU.min).then_inc(s_blk, 1)

            def step(g, c, cm):
                wait(dve, s_bin, c - RING + 1)
                at = bass.ds(c, 1)
                nc.vector.tensor_scalar(lhs_a[:, cm, :], iota0_h[0:EP, :], pos_p[:, at], pay_a[:, at],
                                        ALU.is_equal, ALU.mult)
                nc.vector.tensor_scalar(lhs_b[:, cm, :], iota0_h[0:EP, :], pos_p[:, at], pay_b[:, at],
                                        ALU.is_equal, ALU.mult).then_inc(s_lhs, 1)

            def unpack(g):
                T, t0 = GT[g], B0[g] * U
                dve.wait_ge(s_cum, g + 1)
                nc.vector.tensor_tensor(dif_a[:, 0:T], cum_a[:, 1:T + 1], cum_a[:, 0:T], ALU.subtract)
                link(nc.vector.tensor_tensor(dif_b[:, 0:T], cum_b[:, 1:T + 1], cum_b[:, 0:T], ALU.subtract))
                nc.vector.tensor_scalar(loc_i[:, 0:T], dif_a[:, 0:T], 4, None, ALU.logical_shift_right)
                link(nc.vector.tensor_scalar(dif_b[:, 0:T], dif_b[:, 0:T], 1, None, ALU.logical_shift_right))
                nc.vector.tensor_copy(loc_s[:, t0:t0 + T], loc_i[:, 0:T])
                link(nc.vector.tensor_scalar(dif_a[:, 0:T], dif_a[:, 0:T], 14, 9, ALU.bitwise_and,
                                             ALU.logical_shift_left))
                nc.vector.tensor_tensor(dst_s[:, t0:t0 + T], dif_a[:, 0:T], dif_b[:, 0:T],
                                        ALU.bitwise_or).then_inc(s_sorted, 1)
                dve.wait_ge(s_sorted, g + 1)

            def tiles(g, m, mm):
                n, nm = m + 2, (mm + 2) % 4
                if inside(n, g):
                    wait(dve, s_ot, n - RING + 1)
                    wait(dve, s_of, n - RING + 1)
                    for u in range(U):
                        last = nc.vector.tensor_scalar(oneh[:, nm, u, :], iota1_bf[:, :],
                                                       loc_s[:, bass.ds(n * U + u, 1)], None, ALU.is_equal)
                    last.then_inc(s_oneh, 1)
                n, nm = m, mm
                if inside(n, g):
                    dve.wait_ge(s_kv[nm], (n - nm) * 16 + 16 * U)
                    dve.wait_ge(s_q, n + 1)
                    nc.vector.tensor_tensor(prod[:, nm % 2, :].rearrange("p (u d) -> p u d", u=U),
                                            ps_q[nm % 2][:, 0:U * D].rearrange("p (u d) -> p u d", u=U),
                                            kv[:, nm, :, 0:D], ALU.mult).then_inc(s_prod, 1)
                n, nm = m - 1, (mm - 1) % 4
                if inside(n, g):
                    wait(dve, s_res, n - 1)
                    dve.wait_ge(s_exp, n + 1)
                    nc.vector.tensor_tensor(
                        wv[:, nm % 2, :, 0:D].rearrange("p u (h d) -> p u h d", h=HEADS),
                        kv[:, nm, :, D:2 * D].rearrange("p u (h d) -> p u h d", h=HEADS),
                        wv[:, nm % 2, :, D:RW].unsqueeze(3).to_broadcast([P, U, HEADS, DH]),
                        ALU.mult).then_inc(s_wv, 1)
                n, nm = m, mm
                if inside(n, g):
                    dve.wait_ge(s_prod, n + 1)
                    nc.vector.tensor_reduce(score[:, nm % 2, :],
                                            prod[:, nm % 2, :].rearrange("p (h d) -> p h d", d=DH),
                                            axis=AX.X, op=ALU.add).then_inc(s_score, 1)

                def add_up(us):
                    n, nm = m - 2, (mm - 2) % 4
                    if inside(n, g):
                        for u in us:
                            wait(dve, s_acc, n * U + u)
                            at = acc_b[:, bass.ds(blks[u], 1), :].rearrange("p a d -> p (a d)")
                            nc.vector.tensor_tensor(at, at, ps_r[nm % 2][:, u * RW:(u + 1) * RW],
                                                    ALU.add).then_inc(s_acc, 1)

                if inside(m - 2, g):
                    blks = nc.values_load_multi_w_load_instructions(
                        blk_s[0:1, bass.ds((m - 2) * U, U)], engines=[mybir.EngineType.DVE], min_val=0, max_val=NB - 1,
                        skip_runtime_bounds_check_because="clamped when the table is made")[1]
                    dve.wait_ge(s_res, m - 2 + 1)
                add_up([0, 1])
                n, nm = m, mm
                if inside(n, g):
                    dve.wait_ge(s_score, n + 1)
                    nc.vector.tensor_scalar(clipped[:, nm % 2, :], score[:, nm % 2, :], -10.0, 10.0,
                                            ALU.max, ALU.min).then_inc(s_clip, 1)
                add_up([2, 3])
                woven(g, m, mm, step)

            ranks(0)
            rest_of_sorting(dve, 0, step)
            unpack(0)
            dve.wait_ge(s_acc0, 1)
            for g in range(G):
                if g + 1 < G:
                    ranks(g + 1)
                dve.wait_ge(s_blk, g + 1)
                batches(dve, g, lambda m, mm: tiles(g, m, mm))
                if g + 1 < G:
                    rest_of_sorting(dve, g + 1, step)
                    unpack(g + 1)
            dve.wait_ge(s_acc, NT)
            link(nc.vector.tensor_scalar(den[:, :, :], acc_b[:, :, D:RW], 1e-8, None, ALU.add))
            link(nc.vector.reciprocal(den[:, :, :], den[:, :, :]))
            for i in range(NPC):
                bs = slice(i * PC, (i + 1) * PC)
                y = acc_b[:, bs, 0:D]
                for b in range(i * PC, (i + 1) * PC):
                    yh = acc_b[:, b, 0:D].rearrange("p (h d) -> p h d", h=HEADS)
                    last = nc.vector.tensor_tensor(yh, yh, den[:, b, :].unsqueeze(2).to_broadcast([P, HEADS, DH]),
                                                   ALU.mult)
                link(last)
                dve.wait_ge(s_xe[i % 2], 16 * (i // 2 + 1))
                nx = PC if i < NPC - 1 else PC - 1
                last = nc.vector.scalar_tensor_tensor(y[:, 0:nx, :], xc[:, i % 2, 0:nx, :], 2.0, y[:, 0:nx, :],
                                                      ALU.mult, ALU.add)
                if nx < PC:
                    last = nc.vector.scalar_tensor_tensor(y[:, nx, :], xlast[:, :], 2.0, y[:, nx, :],
                                                          ALU.mult, ALU.add)
                link(last)
                link(nc.vector.tensor_reduce(mean[:, :], y, axis=AX.X, op=ALU.add))
                link(nc.vector.tensor_scalar(mean[:, :], mean[:, :], 1.0 / D, None, ALU.mult))
                nc.vector.tensor_tensor(cent[:, :, :], y, mean[:, :].unsqueeze(2).to_broadcast([P, PC, D]),
                                        ALU.subtract).then_inc(s_cent, 1)
                dve.wait_ge(s_sq, i + 1)
                link(nc.vector.tensor_reduce(var[:, :], sq[:, :, :], axis=AX.X, op=ALU.add))
                nc.vector.tensor_scalar(var[:, :], var[:, :], 1.0 / D, 1e-5, ALU.mult, ALU.add).then_inc(s_var, 1)
                dve.wait_ge(s_std, i + 1)
                link(nc.vector.reciprocal(inv[:, :], std[:, :]))
                if i >= 2:
                    dve.wait_ge(s_out[i % 2], 16 * (i // 2))
                nc.vector.tensor_tensor(yout[:, i % 2, :, :], cent[:, :, :],
                                        inv[:, :].unsqueeze(2).to_broadcast([P, PC, D]),
                                        ALU.mult).then_inc(s_y, 1)
                dve.wait_ge(s_y, i + 1)


_INS = ['x', 'src', 'dst', 'L0_gnn_qW', 'L0_gnn_kW', 'L0_gnn_vW']
_OUTS = [((6250, 96), 'float32')]


def kernel(**inputs):
    import numpy as _np
    import concourse.bacc as _bacc
    from concourse import mybir as _mybir
    from concourse.bass_utils import run_bass_kernel_spmd as _run

    nc = _bacc.Bacc("TRN2", target_bir_lowering=False, num_devices=1)
    arrays, args = {}, []
    for name in _INS:
        a = _np.ascontiguousarray(inputs[name])
        arrays[f"in_{name}_dram"] = a
        args.append(nc.dram_tensor(f"in_{name}_dram", a.shape, _mybir.dt.from_np(a.dtype), kind="ExternalInput").ap())
    for i, (shape, dtype) in enumerate(_OUTS):
        dt = _mybir.dt.from_np(_np.dtype(dtype))
        args.append(nc.dram_tensor(f"out_{i}_dram", shape, dt, kind="ExternalOutput").ap())
    gnn(nc, *args)
    r = _run(nc, [arrays], core_ids=[0])
    got = tuple(r.results[0][f"out_{i}_dram"] for i in range(len(_OUTS)))
    return got[0]
```

```python
import concourse.bass as bass
from concourse import mybir
from contextlib import ExitStack



def gnn(nc, x, src, dst, qW, kW, vW, out):
    f32, i32, u16 = mybir.dt.float32, mybir.dt.int32, mybir.dt.uint16
    f16, bf16 = mybir.dt.float16, mybir.dt.bfloat16
    ALU = mybir.AluOpType
    ACT = mybir.ActivationFunctionType
    AX = mybir.AxisListType

    P = 128
    N, D = x.shape
    E = src.shape[0]
    HEADS = 4
    DH = D // HEADS
    NB = (N + P - 1) // P
    LASTB = N - (NB - 1) * P
    EP, EC = 125, E // 125
    assert EP * EC == E
    RW = D + HEADS
    U = 5
    R = 8
    SU = 10
    L = 6

    GC = [140, 200, 240, 270]
    G = len(GC)
    assert sum(GC) == EC and all(c % SU == 0 for c in GC)
    GT = [-(-((EP * c + NB * (P - 1)) // P) // U) * U for c in GC]
    C0 = [sum(GC[:g]) for g in range(G + 1)]
    V0 = [c // SU for c in C0]
    B0 = [sum(GT[:g]) // U for g in range(G + 1)]
    T0 = [b * U for b in B0]
    NT, NBT = T0[G], B0[G]
    CMAX, TMAX = max(GC), max(GT)
    assert TMAX + 1 <= 512 and P * TMAX < 1 << 16
    PC = 7
    NPC = NB // PC
    assert NPC * PC == NB
    LCH = [[(t, min(t + P, GT[g])) for t in range(0, GT[g], P)] for g in range(G)]

    PLAN = []

    def plan_iters(m, count, woven=None):
        end = m + count
        looped = max(m, R)
        if woven:
            looped = max(looped, m + 2)
        last = min(end, NBT - L)
        if woven:
            last = min(last, end - 1)
        last = looped + max(0, last - looped) // R * R
        for kind, a, b in (("iters", m, min(looped, end)), ("loop", looped, last), ("iters", max(last, m), end)):
            if b > a and not (kind == "iters" and a == m and b == end and PLAN[-1][1:3] == (a, b)):
                PLAN.append((kind, a, b, woven and (woven[0], woven[1] + a - m)))
        return end

    def plan():
        RANK = ("mark", "count", "place0", "place1", "own")
        PLAN.append(("piece", "project", 0))
        for name in RANK:
            PLAN.append(("piece", name, 0))
        PLAN.append(("sort", 0))
        PLAN.append(("piece", "unpack", 0))
        m = plan_iters(-L, L)
        for g in range(G - 1):
            units = V0[g + 2] - V0[g + 1]
            spare = B0[g + 1] - L - m - (units + 1)
            assert spare >= 0
            for k, name in enumerate(RANK):
                PLAN.append(("piece", name, g + 1))
                m = plan_iters(m, (k + 1) * spare // len(RANK) - k * spare // len(RANK))
            m = plan_iters(m, units + 1, (g + 1, V0[g + 1]))
            PLAN.append(("piece", "unpack", g + 1))
        plan_iters(m, NBT + 2 - m)

    plan()

    kv_dram = nc.dram_tensor("kv_table", [NB * P, 2 * D], f32).ap()
    loc_dram = nc.dram_tensor("loc_rows", [NT, P], bf16).ap()

    with ExitStack() as ctx:
        def sb(name, shape, dt):
            return ctx.enter_context(nc.sbuf_tensor(name, shape, dt))

        def pb(name, shape, dt):
            return ctx.enter_context(nc.psum_tensor(name, shape, dt))

        def sem(name):
            return ctx.enter_context(nc.semaphore(name))

        iota_i = sb("iota_i", [P, TMAX + 1], i32)
        iota_f = sb("iota_f", [P, TMAX + 1], f32)
        iota_s = sb("iota_s", [P, P, SU], f16)
        iota_u = sb("iota_u", [P, NB], u16)
        part_i = sb("part_i", [P, 1], i32)
        part_f = sb("part_f", [P, 1], f32)
        part1_f = sb("part1_f", [P, 1], f32)
        ident_f = sb("ident_f", [P, P], f32)
        ident_bf = sb("ident_bf", [P, P], bf16)
        tri_h = sb("tri_h", [P, P], f16)
        ones_h = sb("ones_h", [P, P], f16)
        ident_h = sb("ident_h", [P, P], f16)
        w_all = sb("w_all", [D, 3 * D], f32)
        xlast = sb("xlast", [P, D], f32)
        q3 = sb("q3", [P, 3, NB, D], bf16)
        acc = sb("acc", [P, NB, RW], f32)
        src_i = sb("src_i", [EP, EC], i32)
        dst_i = sb("dst_i", [EP, EC], i32)
        tmp_i = sb("tmp_i", [EP, CMAX], i32)
        bin_u = sb("bin_u", [EP, CMAX], u16)
        pay_a = sb("pay_a", [EP, EC], f16)
        pay_b = sb("pay_b", [EP, EC], f16)
        pos_p = sb("pos_p", [EP, EC], f16)
        pos_t = sb("pos_t", [EP, EC], f32)
        steps_m = sb("steps_m", [EP, NB * (CMAX + 2)], f16)
        place_m = sb("place_m", [EP, NB * (CMAX + 2)], u16)
        cnt_f = sb("cnt_f", [EP, NB], f32)
        cnt = sb("cnt", [EP, NB], f16)
        step_i = sb("step_i", [EP, NB], i32)
        step_lo = sb("step_lo", [EP, NB], i32)
        need_i = sb("need_i", [P, NB], i32)
        need = sb("need", [P, NB], f32)
        tend = sb("tend", [P, NB], f32)
        tdiag = sb("tdiag", [P, NB], f32)
        tend_p = sb("tend_p", [P, 1], f32)
        after = sb("after", [P, TMAX], f16)
        firstp = sb("firstp", [P, NB], f32)
        endp = sb("endp", [P, NB], f32)
        LW = P * SU
        lhs_m = place_m[:, 0:5 * LW].bitcast(f16)
        lhs_1 = lhs_m[:, 0:LW].rearrange("p (q c) -> p q c", c=SU)
        lhs_a = lhs_m[:, LW:3 * LW].rearrange("p (i q c) -> p i q c", i=2, c=SU)
        lhs_b = lhs_m[:, 3 * LW:5 * LW].rearrange("p (i q c) -> p i q c", i=2, c=SU)
        theta = steps_m[:, 0:2 * SU * (TMAX + 1)].rearrange("p (i c t) -> p i c t", i=2, c=SU)
        cum_a = sb("cum_a", [P, TMAX + 1], f32)
        cum_b = sb("cum_b", [P, TMAX + 1], f32)
        dif_a = sb("dif_a", [P, TMAX], i32)
        dif_b = iota_i
        dst_s = sb("dst_s", [P, NT], i32)
        loc_s = sb("loc_s", [P, TMAX], bf16)
        loc_t = sb("loc_t", [P, 4, P], bf16)
        blk_s = sb("blk_s", [1, NT], i32)
        idx = sb("idx", [P, R, U], i32)
        kv = sb("kv", [P, R, U, 2 * D], f32)
        loc_b = sb("loc_b", [P, R, U * P], bf16)
        onehT = sb("onehT", [P, 4, U * P], bf16)
        oneh = sb("oneh", [P, 2, U, P], f32)
        prod = sb("prod", [P, 2, U * D], f32)
        score = sb("score", [P, 2, U * HEADS], f32)
        clipped = sb("clipped", [P, 2, U * HEADS], f32)
        wv = sb("wv", [P, 2, U, RW], f32)
        den = sb("den", [P, NB, HEADS], f32)
        mean = sb("mean", [P, 2, PC], f32)
        var = sb("var", [P, 2, PC], f32)
        std = sb("std", [P, 2, PC], f32)
        inv = sb("inv", [P, 2, PC], f32)

        kv_m = kv[:, :, :, :].rearrange("p r u d -> p (r u d)")
        loc_m = loc_b[:, :, :].rearrange("p r e -> p (r e)").bitcast(f32)
        CH = PC * D
        stg = kv_m[:, 0:2 * 3 * CH].rearrange("p (i b d) -> p i b d", i=2, d=3 * D)
        xc = loc_m[:, 0:2 * CH].rearrange("p (i b d) -> p i b d", i=2, d=D)
        xT = loc_m[0:D, 2 * CH:2 * CH + PC * P].rearrange("p (b n) -> p b n", n=P)

        def end_buf(i):
            return kv_m[:, i * CH:(i + 1) * CH].rearrange("p (b d) -> p b d", d=D)

        xe = [end_buf(0), end_buf(1)]
        cent = [end_buf(2), end_buf(3)]
        sq = [end_buf(4), end_buf(5)]
        yout = [end_buf(6), end_buf(7)]

        ps_a = pb("ps_a", [P, 512], f32)
        ps_b = pb("ps_b", [P, 512], f32)
        ps_t = [pb(f"ps_t{i}", [P, 512], f32) for i in range(2)]
        ps_q = [pb(f"ps_q{i}", [P, 512], f32) for i in range(2)]
        ps_r = [pb(f"ps_r{i}", [P, 512], f32) for i in range(2)]
        ps_p = ps_r + ps_t

        s_x = [sem("s_x0"), sem("s_x1")]
        s_xe = [sem("s_xe0"), sem("s_xe1")]
        s_xl = sem("s_xl")
        s_w = sem("s_w")
        s_src = sem("s_src")
        s_dst = sem("s_dst")
        s_iota = sem("s_iota")
        s_const = sem("s_const")
        s_xpad = sem("s_xpad")
        s_xt = sem("s_xt")
        s_xtc = sem("s_xtc")
        s_prj = sem("s_prj")
        s_prjc = sem("s_prjc")
        s_kvst = [sem("s_kvst0"), sem("s_kvst1")]
        s_hi = sem("s_hi")
        s_r1 = sem("s_r1")
        s_mid = sem("s_mid")
        s_lo = sem("s_lo")
        s_own = sem("s_own")
        s_mark = sem("s_mark")
        s_tally = sem("s_tally")
        s_cnt = sem("s_cnt")
        s_pre = sem("s_pre")
        s_after = sem("s_after")
        s_tab = sem("s_tab")
        s_blk = sem("s_blk")
        s_pos = sem("s_pos")
        s_lhs = sem("s_lhs")
        s_theta = sem("s_theta")
        s_bin = sem("s_bin")
        s_cum = sem("s_cum")
        s_sorted = sem("s_sorted")
        s_loc = sem("s_loc")
        s_loct = sem("s_loct")
        s_loctc = sem("s_loctc")
        s_locw = sem("s_locw")
        s_locb = [sem(f"s_locb{i}") for i in range(R)]
        s_acc0 = sem("s_acc0")
        s_idx = sem("s_idx")
        s_kv = [sem(f"s_kv{i}") for i in range(R)]
        s_oneT = sem("s_oneT")
        s_ot = sem("s_ot")
        s_one = sem("s_one")
        s_q = sem("s_q")
        s_prod = sem("s_prod")
        s_score = sem("s_score")
        s_clip = sem("s_clip")
        s_exp = sem("s_exp")
        s_wv = sem("s_wv")
        s_res = sem("s_res")
        s_acc = sem("s_acc")
        s_den = sem("s_den")
        s_div = sem("s_div")
        s_cent = sem("s_cent")
        s_sq = sem("s_sq")
        s_var = sem("s_var")
        s_std = sem("s_std")
        s_inv = sem("s_inv")
        s_y = sem("s_y")
        s_out = [sem("s_out0"), sem("s_out1")]
        s_past = sem("s_past")

        def wait(eng, s, v):
            if not (isinstance(v, int) and v <= 0):
                eng.wait_ge(s, v)

        def follow(eng, tiles, unit, pieces):
            for what in PLAN:
                if what[0] == "piece":
                    if what[1] in pieces:
                        pieces[what[1]](what[2])
                elif what[0] == "sort":
                    sort_stretch(eng, unit, what[1])
                else:
                    kind, m0, m1, woven = what
                    g, v = woven or (0, 0)
                    v -= eng is nc.tensor
                    if kind == "iters":
                        for m in range(m0, m1):
                            tiles(m, m % R)
                            if woven and unit and V0[g] <= v + m - m0 < V0[g + 1]:
                                unit(g, v + m - m0, (v + m - m0) % 2)
                    else:
                        with eng.Fori(m0, m1 - R + 1, R) as i:
                            for k in range(R):
                                tiles(i + k, (m0 + k) % R)
                                if woven and unit:
                                    unit(g, i + (k + v - m0), (v + k) % 2)

        def sort_stretch(eng, unit, g):
            if not unit:
                return
            v0, v1 = V0[g], V0[g + 1]
            a = min(v1, v0 + 2)
            b = a + max(0, v1 - 1 - a) // 2 * 2
            for v in range(v0, a):
                unit(g, v, v % 2)
            if b > a:
                with eng.Fori(a, b - 1, 2) as i:
                    for k in range(2):
                        unit(g, i + k, (a + k) % 2)
            for v in range(b, v1):
                unit(g, v, v % 2)

        def there(n):
            return not isinstance(n, int) or 0 <= n < NBT

        def blocks_of(engine, n):
            return nc.values_load_multi_w_load_instructions(
                blk_s[0:1, bass.ds(n * U, U)], engines=[engine], min_val=0, max_val=NB - 1,
                skip_runtime_bounds_check_because="clamped when the table is made")[1]

        block = ctx.enter_context(nc.Block())

        @block.sync
        def _(sp):
            def load_x(i, to, slot_sem):
                n = PC if i < NPC - 1 else PC - 1
                sp.dma_start(to[:, 0:n, :],
                             x[i * PC * P:(i * PC + n) * P, :].rearrange("(b p) d -> p b d", p=P)).then_inc(slot_sem, 16)

            sp.dma_start(src_i[:, :], src.rearrange("(p c) -> p c", c=EC)).then_inc(s_src, 16)
            load_x(0, xc[:, 0], s_x[0])
            for i, w in enumerate((qW, kW, vW)):
                sp.dma_start(w_all[:, i * D:(i + 1) * D], w).then_inc(s_w, 16)
            load_x(1, xc[:, 1], s_x[1])
            sp.dma_start(dst_i[:, :], dst.rearrange("(p c) -> p c", c=EC)).then_inc(s_dst, 16)
            sp.wait_ge(s_xpad, 1)
            sp.dma_start(xlast[0:LASTB, :], x[(NB - 1) * P:N, :]).then_inc(s_xl, 16)
            kv_rows = kv_dram.rearrange("(i b p) d -> i p b d", p=P, b=PC)
            for i in range(NPC):
                if i + 2 < NPC:
                    sp.wait_ge(s_xt, 2 * i + 2)
                    load_x(i + 2, xc[:, i % 2], s_x[i % 2])
                sp.wait_ge(s_prjc, PC * (i + 1))
                sp.dma_start(kv_rows[i], stg[:, i % 2, :, D:3 * D]).then_inc(s_kvst[i % 2], 16)

            written = 0
            for g in range(G):
                for k, (a, b) in enumerate(LCH[g]):
                    if k == 0:
                        sp.wait_ge(s_loctc, g + 1)
                    sp.dma_start(loc_dram[T0[g] + a:T0[g] + b, :], loc_t[0:b - a, k, :]).then_inc(s_locw, 16)
                    written += 16
                sp.wait_ge(s_locw, written)

                def load_rows(n, nm):
                    wait(sp, s_oneT, n - R + 1)
                    sp.dma_start(loc_b[:, nm, :],
                                 loc_dram[bass.ds(n * U, U), :].rearrange("t e -> (t e)").partition_broadcast(P)
                                 ).then_inc(s_locb[nm], 16)

                lo, hi = B0[g], B0[g + 1]
                a = max(lo, R)
                b = a + (hi - a) // R * R
                for n in range(lo, a):
                    load_rows(n, n % R)
                with sp.Fori(a, b - R + 1, R) as i:
                    for k in range(R):
                        load_rows(i + k, (a + k) % R)
                for n in range(b, hi):
                    load_rows(n, n % R)

            sp.wait_ge(s_acc, NT)
            load_x(0, xe[0], s_xe[0])
            load_x(1, xe[1], s_xe[1])
            for i in range(NPC):
                sp.wait_ge(s_y, i + 1)
                y = yout[i % 2]
                if i < NPC - 1:
                    sp.dma_start(out[i * PC * P:(i + 1) * PC * P, :].rearrange("(b p) d -> p b d", p=P),
                                 y).then_inc(s_out[i % 2], 16)
                else:
                    sp.dma_start(out[i * PC * P:(NB - 1) * P, :].rearrange("(b p) d -> p b d", p=P),
                                 y[:, 0:PC - 1, :]).then_inc(s_out[i % 2], 16)
                    sp.dma_start(out[(NB - 1) * P:N, :], y[0:LASTB, PC - 1, :]).then_inc(s_out[i % 2], 16)
                if i + 2 < NPC:
                    load_x(i + 2, xe[i % 2], s_xe[i % 2])
            last = (NPC - 1) % 2
            sp.wait_ge(s_out[last], 16 * ((NPC + 1) // 2 + 1))
            sp.wait_ge(s_out[1 - last], 16 * (NPC // 2))

        @block.gpsimd
        def _(pool):
            nc.gpsimd.iota(iota_i[:, :], [[1, TMAX + 1]], base=0, channel_multiplier=0).then_inc(s_iota, 1)
            nc.gpsimd.iota(part_i[:, :], [[1, 1]], base=0, channel_multiplier=1).then_inc(s_iota, 1)
            nc.gpsimd.memset(ones_h[:, :], 1.0).then_inc(s_iota, 1)
            nc.gpsimd.memset(xlast[:, :], 0.0).then_inc(s_xpad, 1)
            nc.gpsimd.memset(acc[:, :, :], 0.0).then_inc(s_acc0, 1)
            for i in range(NPC):
                bs = slice(i * PC, (i + 1) * PC)
                qs = stg[:, i % 2, :, 0:D]
                pool.wait_ge(s_hi, i + 1)
                nc.gpsimd.tensor_tensor(qs, qs, q3[:, 0, bs, :], ALU.subtract).then_inc(s_r1, 1)
                pool.wait_ge(s_mid, i + 1)
                nc.gpsimd.tensor_tensor(q3[:, 2, bs, :], qs, q3[:, 1, bs, :], ALU.subtract).then_inc(s_lo, 1)
            pool.wait_ge(s_kvst[0], 16 * ((NPC + 1) // 2))
            pool.wait_ge(s_kvst[1], 16 * (NPC // 2))
            pool.wait_ge(s_lo, NPC)

            def tiles(m, mm):
                n, nm = m + L, (mm + L) % R
                if there(n):
                    pool.wait_ge(s_idx, n + 1)
                    pool.sem_inc(s_past, 1)
                    for u in range(U):
                        nc.gpsimd.indirect_dma_start(
                            kv[:, nm, u, :], None, kv_dram,
                            bass.IndirectOffsetOnAxis(ap=idx[:, nm, u:u + 1], axis=0)).then_inc(s_kv[nm], 16)

            follow(pool, tiles, None, {})
            for i in range(NPC + 2):
                if i < NPC:
                    y = acc[:, i * PC:(i + 1) * PC, 0:D].rearrange("p b (h d) -> p b h d", h=HEADS)
                    pool.wait_ge(s_den, 1)
                    nc.gpsimd.tensor_tensor(y, y, den[:, i * PC:(i + 1) * PC, :].unsqueeze(3)
                                            .to_broadcast([P, PC, HEADS, DH]), ALU.mult).then_inc(s_div, 1)
                if i >= 2:
                    j = i - 2
                    pool.wait_ge(s_inv, j + 1)
                    if j >= 2:
                        pool.wait_ge(s_out[j % 2], 16 * (j // 2))
                    nc.gpsimd.tensor_tensor(yout[j % 2], cent[j % 2],
                                            inv[:, j % 2, :].unsqueeze(2).to_broadcast([P, PC, D]),
                                            ALU.mult).then_inc(s_y, 1)

        @block.tensor
        def _(pe):
            def project(_):
                for i in range(NPC):
                    pe.wait_ge(s_x[i % 2], 16 * (i // 2 + 1))
                    if i == 0:
                        pe.wait_ge(s_const, 1)
                    if i == NPC - 1:
                        pe.wait_ge(s_xl, 16)
                    for h, (a, b) in enumerate(((0, 4), (4, PC))):
                        wait(pe, s_xtc, 2 * i + h - 1)
                        for j in range(a, b):
                            xb = xlast[:, :] if i * PC + j == NB - 1 else xc[:, i % 2, j, :]
                            last = nc.tensor.transpose(ps_q[h][0:D, (j - a) * P:(j - a + 1) * P], xb, ident_f[:, :])
                        last.then_inc(s_xt, 1)
                    for j in range(PC):
                        b = i * PC + j
                        if j == 0 or j == 4:
                            pe.wait_ge(s_xtc, 2 * i + 1 + (j == 4))
                        if j == 0 and i == 0:
                            pe.wait_ge(s_w, 48)
                        wait(pe, s_prjc, b - 3)
                        nc.tensor.matmul(ps_p[b % 4][:, 0:3 * D], xT[:, j, :], w_all[:, :],
                                         start=True, stop=True).then_inc(s_prj, 1)

            def mark(g):
                C = GC[g]
                steps = steps_m[:, 0:NB * (C + 2)].rearrange("p (b c) -> p b c", b=NB)
                pe.wait_ge(s_mark, g + 1)
                wait(pe, s_loctc, g)
                for c in range(0, C, SU):
                    last = nc.tensor.matmul(ps_a[0:EP, 0:NB * SU], ident_h[0:EP, 0:EP],
                                            steps[:, :, 2 + c:2 + c + SU], start=c == 0, stop=c == C - SU)
                last.then_inc(s_tally, 1)

            def count(g):
                pe.wait_ge(s_cnt, g + 1)
                nc.tensor.matmul(ps_a[:, 0:NB], tri_h[0:EP, :], cnt[:, :], start=True, stop=True)
                nc.tensor.matmul(ps_a[:, 64:64 + NB], ones_h[0:EP, :], cnt[:, :],
                                 start=True, stop=True).then_inc(s_pre, 1)
                pe.wait_ge(s_after, g + 1)
                nc.tensor.matmul(ps_a[:, 0:GT[g]], ones_h[:, :], after[:, 0:GT[g]],
                                 start=True, stop=True).then_inc(s_tab, 1)

            def unit(g, v, vm):
                w = GT[g] + 1
                first = isinstance(v, int) and v == V0[g]
                last = isinstance(v, int) and v == V0[g + 1] - 1
                if first:
                    pe.wait_ge(s_blk, g + 1)
                pe.wait_ge(s_lhs, v + 1)
                pe.wait_ge(s_theta, v + 1)
                for j in range(SU):
                    for ps, lhs in ((ps_a, lhs_a), (ps_b, lhs_b)):
                        mm = nc.tensor.matmul(ps[:, 0:w], lhs[:, vm, :, j], theta[:, vm, j, 0:w],
                                              start=first and j == 0, stop=last and j == SU - 1)
                mm.then_inc(s_bin, 1)

            def unpack(g):
                pe.wait_ge(s_loc, g + 1)
                for k, (a, b) in enumerate(LCH[g]):
                    last = nc.tensor.transpose(ps_a[0:b - a, k * P // 2:(k + 1) * P // 2].bitcast(bf16),
                                               loc_s[:, a:b], ident_bf[:, :])
                last.then_inc(s_loct, 1)

            def tiles(m, mm):
                n, nm = m + 1, (mm + 1) % R
                if there(n):
                    blks = blocks_of(mybir.EngineType.PE, n)
                    pe.wait_ge(s_oneT, n + 1)
                    wait(pe, s_prod, n - 1)
                    for u in range(U):
                        for i in range(3):
                            last = nc.tensor.matmul(ps_q[nm % 2][:, u * D:(u + 1) * D],
                                                    onehT[:, nm % 4, u * P:(u + 1) * P],
                                                    q3[:, i, bass.ds(blks[u], 1), :].rearrange("p a d -> p (a d)"),
                                                    start=(i == 0), stop=(i == 2))
                    last.then_inc(s_q, 1)
                n, nm = m, mm
                if there(n):
                    wait(pe, s_one, n - 1)
                    for u in range(U):
                        last = nc.tensor.transpose(ps_t[nm % 2][:, u * P // 2:(u + 1) * P // 2].bitcast(bf16),
                                                   onehT[:, nm % 4, u * P:(u + 1) * P], ident_bf[:, :])
                    last.then_inc(s_ot, 1)
                n, nm = m - 1, (mm - 1) % R
                if there(n):
                    pe.wait_ge(s_one, n + 1)
                    pe.wait_ge(s_wv, n + 1)
                    wait(pe, s_acc, U * (n - 1))
                    for u in range(U):
                        last = nc.tensor.matmul(ps_r[nm % 2][:, u * RW:(u + 1) * RW], oneh[:, nm % 2, u, :],
                                                wv[:, nm % 2, u, :], start=True, stop=True)
                    last.then_inc(s_res, 1)

            follow(pe, tiles, unit, {"project": project, "mark": mark, "count": count, "unpack": unpack})

        @block.scalar
        def _(act):
            def project(_):
                for i in range(NPC):
                    for h, (a, b) in enumerate(((0, 4), (4, PC))):
                        act.wait_ge(s_xt, 2 * i + h + 1)
                        wait(act, s_prj, (i - 1) * PC + b)
                        nc.scalar.activation(xT[:, a:b, :].rearrange("p b n -> p (b n)"),
                                             ps_q[h][0:D, 0:(b - a) * P], ACT.Copy).then_inc(s_xtc, 1)
                    if i >= 2:
                        act.wait_ge(s_lo, i - 1)
                        act.wait_ge(s_kvst[i % 2], 16 * (i // 2))
                    for j in range(PC):
                        b = i * PC + j
                        act.wait_ge(s_prj, b + 1)
                        nc.scalar.activation(stg[:, i % 2, j, :], ps_p[b % 4][:, 0:3 * D],
                                             ACT.Copy).then_inc(s_prjc, 1)
                    bs = slice(i * PC, (i + 1) * PC)
                    act.wait_ge(s_prjc, PC * (i + 1))
                    nc.scalar.activation(q3[:, 0, bs, :], stg[:, i % 2, :, 0:D], ACT.Copy).then_inc(s_hi, 1)
                    if i:
                        split_mid(i - 1)
                split_mid(NPC - 1)

            def split_mid(i):
                act.wait_ge(s_r1, i + 1)
                nc.scalar.activation(q3[:, 1, i * PC:(i + 1) * PC, :], stg[:, i % 2, :, 0:D],
                                     ACT.Copy).then_inc(s_mid, 1)

            def unit(g, v, vm):
                if isinstance(v, int) and v == V0[g]:
                    act.wait_ge(s_pos, g + 1)
                wait(act, s_bin, v - 1)
                act.sem_inc(s_past, 1)
                w = GT[g] + 1
                for j in range(SU):
                    last = nc.scalar.activation(theta[:, vm, j, 0:w], iota_f[0:EP, 0:w], ACT.Sign,
                                                bias=pos_t[:, bass.ds(v * SU + j, 1)])
                last.then_inc(s_theta, 1)

            def unpack(g):
                w = GT[g] + 1
                act.wait_ge(s_bin, V0[g + 1])
                wait(act, s_sorted, g)
                nc.scalar.activation(cum_a[:, 0:w], ps_a[:, 0:w], ACT.Copy)
                nc.scalar.activation(cum_b[:, 0:w], ps_b[:, 0:w], ACT.Copy).then_inc(s_cum, 1)
                act.wait_ge(s_loct, g + 1)
                if g:
                    act.wait_ge(s_locw, 16 * sum(len(LCH[h]) for h in range(g)))
                for k, (a, b) in enumerate(LCH[g]):
                    last = nc.scalar.activation(loc_t[0:b - a, k, :],
                                                ps_a[0:b - a, k * P // 2:(k + 1) * P // 2].bitcast(bf16), ACT.Copy)
                last.then_inc(s_loctc, 1)
                act.wait_ge(s_sorted, g + 1)

            def tiles(m, mm):
                n, nm = m, mm
                if there(n):
                    wait(act, s_res, n - 1)
                    act.wait_ge(s_ot, n + 1)
                    nc.scalar.activation(oneh[:, nm % 2, :, :].rearrange("p u n -> p (u n)"),
                                         ps_t[nm % 2][:, 0:U * P // 2].bitcast(bf16), ACT.Copy).then_inc(s_one, 1)
                    act.wait_ge(s_clip, n + 1)
                    nc.scalar.activation(wv[:, nm % 2, :, D:RW],
                                         clipped[:, nm % 2, :].rearrange("p (u h) -> p u h", h=HEADS),
                                         ACT.Exp).then_inc(s_exp, 1)
                n, nm = m + L, (mm + L) % R
                if there(n):
                    stage(n, nm)

            def stage(n, nm):
                wait(act, s_wv, n - R + 1)
                act.sem_inc(s_past, 1)
                nc.scalar.activation(idx[:, nm, :], dst_s[:, bass.ds(n * U, U)], ACT.Copy).then_inc(s_idx, 1)

            follow(act, tiles, unit, {"project": project, "unpack": unpack})
            for i in range(NPC):
                act.wait_ge(s_cent, i + 1)
                nc.scalar.activation(sq[i % 2], cent[i % 2], ACT.Square).then_inc(s_sq, 1)
                act.wait_ge(s_var, i + 1)
                nc.scalar.activation(std[:, i % 2, :], var[:, i % 2, :], ACT.Sqrt).then_inc(s_std, 1)

        @block.vector
        def _(dve):
            own = [0]

            def link(ins):
                own[0] += 1
                ins.then_inc(s_own, 1)
                dve.wait_ge(s_own, own[0])

            dve.wait_ge(s_iota, 3)
            nc.vector.tensor_copy(iota_f[:, :], iota_i[:, :])
            nc.vector.tensor_copy(iota_u[:, :], iota_i[:, 0:NB])
            link(nc.vector.tensor_copy(part_f[:, :], part_i[:, :]))
            nc.vector.tensor_scalar(part1_f[:, :], part_f[:, :], 1.0, None, ALU.add)
            nc.vector.tensor_scalar(ident_bf[:, :], iota_f[:, 0:P], part_f[:, 0:1], None, ALU.is_equal)
            nc.vector.tensor_scalar(ident_h[:, :], iota_f[:, 0:P], part_f[:, 0:1], None, ALU.is_equal)
            nc.vector.tensor_scalar(tri_h[:, :], iota_f[:, 0:P], part_f[:, 0:1], None, ALU.is_gt)
            nc.vector.tensor_scalar(ident_f[:, :], iota_f[:, 0:P], part_f[:, 0:1], None,
                                    ALU.is_equal).then_inc(s_const, 1)
            dve.wait_ge(s_const, 1)

            def group_views(g):
                C = GC[g]
                return (C, steps_m[:, 0:NB * (C + 2)].rearrange("p (b c) -> p b c", b=NB),
                        place_m[:, 0:NB * (C + 2)].rearrange("p (b c) -> p b c", b=NB))

            HALF = (NB + 1) // 2

            def mark(g):
                C, c0, c1 = GC[g], C0[g], C0[g + 1]
                s, d, t = src_i[:, c0:c1], dst_i[:, c0:c1], tmp_i[:, 0:C]
                _, steps, _ = group_views(g)
                if g == 0:
                    dve.wait_ge(s_src, 16)
                link(nc.vector.tensor_scalar(t, s, 7, None, ALU.logical_shift_right))
                link(nc.vector.tensor_copy(bin_u[:, 0:C], t))
                nc.vector.tensor_tensor(steps[:, :, 2:C + 2],
                                        bin_u[:, 0:C].unsqueeze(1).to_broadcast([EP, NB, C]),
                                        iota_u[0:EP, :].unsqueeze(2).to_broadcast([EP, NB, C]),
                                        ALU.is_equal).then_inc(s_mark, 1)
                if g == 0:
                    dve.wait_ge(s_dst, 16)
                link(nc.vector.tensor_scalar(s, s, P - 1, 3, ALU.bitwise_and, ALU.logical_shift_left))
                link(nc.vector.tensor_scalar(t, d, 10, None, ALU.logical_shift_right))
                link(nc.vector.scalar_tensor_tensor(pay_a[:, c0:c1], s, 8.0, t, ALU.add, ALU.add))
                link(nc.vector.tensor_scalar(t, d, 1023, None, ALU.bitwise_and))
                link(nc.vector.tensor_copy(pay_b[:, c0:c1], t))

            def count(g):
                C, steps, _ = group_views(g)
                dve.wait_ge(s_tally, g + 1)
                link(nc.vector.tensor_reduce(cnt_f[:, :], ps_a[0:EP, 0:NB * SU].rearrange("p (b c) -> p b c", c=SU),
                                             axis=AX.X, op=ALU.add))
                nc.vector.tensor_copy(cnt[:, :], cnt_f[:, :]).then_inc(s_cnt, 1)
                dve.wait_ge(s_pre, g + 1)
                link(nc.vector.tensor_scalar(need_i[:, :], ps_a[:, 64:64 + NB], float(P - 1), None, ALU.add))
                link(nc.vector.tensor_scalar(need_i[:, :], need_i[:, :], 7, None, ALU.logical_shift_right))
                link(nc.vector.tensor_copy(need[:, :], need_i[:, :]))
                link(nc.vector.tensor_tensor_scan(tend[:, :], need[:, :], need[:, :], 0.0, ALU.add, ALU.max))
                link(nc.vector.tensor_tensor(tdiag[:, :], tend[:, :], ident_f[:, 0:NB], ALU.mult))
                link(nc.vector.tensor_reduce(tend_p[:, :], tdiag[:, :], axis=AX.X, op=ALU.add))
                link(nc.vector.tensor_tensor(need[:, :], tend[:, :], need[:, :], ALU.subtract))
                link(nc.vector.scalar_tensor_tensor(firstp[:, :], need[:, :], float(P), ps_a[:, 0:NB],
                                                    ALU.mult, ALU.add))
                nc.vector.tensor_scalar(after[:, 0:GT[g]], iota_f[:, 0:GT[g]], tend_p[:, 0:1], None,
                                        ALU.is_ge).then_inc(s_after, 1)
                link(nc.vector.tensor_tensor(endp[0:EP, :], firstp[0:EP, :], cnt_f[:, :], ALU.add))
                nc.vector.tensor_copy(step_i[:, 0:1], firstp[0:EP, 0:1])
                link(nc.vector.tensor_tensor(step_i[:, 1:NB], firstp[0:EP, 1:NB], endp[0:EP, 0:NB - 1],
                                             ALU.subtract))
                link(nc.vector.tensor_scalar(step_lo[:, :], step_i[:, :], 1023, None, ALU.bitwise_and))
                nc.vector.tensor_copy(steps[:, :, 1], step_lo[:, :])
                link(nc.vector.tensor_tensor(steps[:, :, 0], step_i[:, :], step_lo[:, :], ALU.subtract))
                dve.wait_ge(s_tab, g + 1)
                nc.vector.tensor_scalar(blk_s[0:1, T0[g]:T0[g + 1]], ps_a[0:1, 0:GT[g]], float(NB - P),
                                        float(NB - 1), ALU.add, ALU.min).then_inc(s_blk, 1)

            def place(g, b0, b1):
                C, steps, pl = group_views(g)
                a, b = b0 * (C + 2), b1 * (C + 2)
                link(nc.vector.tensor_tensor_scan(place_m[:, a:b], steps_m[:, a:b], steps_m[:, a:b],
                                                  0.0 if b0 == 0 else endp[0:EP, b0 - 1:b0], ALU.add, ALU.max))
                link(nc.vector.tensor_tensor(pl[:, b0:b1, 2:C + 2], pl[:, b0:b1, 2:C + 2],
                                             steps[:, b0:b1, 2:C + 2], ALU.mult))

            def place0(g):
                place(g, 0, HALF)

            def place1(g):
                place(g, HALF, NB)

            def own_position(g):
                C, _, pl = group_views(g)
                c0, c1 = C0[g], C0[g + 1]
                n = NB
                while n > 1:
                    h = n // 2
                    link(nc.vector.tensor_tensor(pl[:, 0:h, 2:C + 2], pl[:, 0:h, 2:C + 2],
                                                 pl[:, n - h:n, 2:C + 2], ALU.add))
                    n -= h
                t, s = tmp_i[:, 0:C], src_i[:, c0:c1]
                link(nc.vector.tensor_scalar(t, pl[:, 0, 2:C + 2], -1.0, None, ALU.add))
                link(nc.vector.tensor_scalar(s, t, P - 1, None, ALU.bitwise_and))
                link(nc.vector.tensor_copy(pos_p[:, c0:c1], s))
                link(nc.vector.tensor_scalar(t, t, 7, None, ALU.logical_shift_right))
                nc.vector.tensor_scalar(pos_t[:, c0:c1], t, -1.0, -0.5, ALU.mult, ALU.add).then_inc(s_pos, 1)
                dve.wait_ge(s_pos, g + 1)
                if g == 0:
                    link(nc.vector.tensor_copy(iota_s[:, :, :],
                                               iota_f[:, 0:P].unsqueeze(2).to_broadcast([P, P, SU])))

            def unit(g, v, vm):
                wait(dve, s_bin, v - 1)
                cols = bass.ds(v * SU, SU)

                def spread(a):
                    return a[:, cols].unsqueeze(1).to_broadcast([EP, P, SU])

                wait(dve, s_lhs, v)
                nc.vector.tensor_tensor(lhs_1[:, :, :], iota_s[0:EP, :, :], spread(pos_p),
                                        ALU.is_equal).then_inc(s_one_lhs, 1)
                dve.wait_ge(s_one_lhs, v + 1)
                nc.vector.tensor_tensor(lhs_a[:, vm, :, :], lhs_1[:, :, :], spread(pay_a), ALU.mult)
                nc.vector.tensor_tensor(lhs_b[:, vm, :, :], lhs_1[:, :, :], spread(pay_b),
                                        ALU.mult).then_inc(s_lhs, 1)

            s_one_lhs = sem("s_one_lhs")

            def unpack(g):
                T, t0 = GT[g], T0[g]
                dve.wait_ge(s_cum, g + 1)
                link(nc.vector.tensor_tensor(dif_a[:, 0:T], cum_a[:, 1:T + 1], cum_a[:, 0:T], ALU.subtract))
                link(nc.vector.tensor_scalar(dif_b[:, 0:T], dif_a[:, 0:T], 4, None, ALU.logical_shift_right))
                link(nc.vector.tensor_copy(loc_s[:, 0:T], dif_b[:, 0:T]))
                link(nc.vector.tensor_scalar(dif_a[:, 0:T], dif_a[:, 0:T], 14, 9, ALU.bitwise_and,
                                             ALU.logical_shift_left))
                nc.vector.tensor_tensor(dif_b[:, 0:T], cum_b[:, 1:T + 1], cum_b[:, 0:T],
                                        ALU.subtract).then_inc(s_loc, 1)
                dve.wait_ge(s_loc, g + 1)
                link(nc.vector.tensor_scalar(dif_b[:, 0:T], dif_b[:, 0:T], 1, None, ALU.logical_shift_right))
                nc.vector.tensor_tensor(dst_s[:, t0:t0 + T], dif_a[:, 0:T], dif_b[:, 0:T],
                                        ALU.bitwise_or).then_inc(s_sorted, 1)
                dve.wait_ge(s_sorted, g + 1)
                if g == 0:
                    dve.wait_ge(s_acc0, 1)

            def tiles(m, mm):
                def add_up(u):
                    n, nm = m - 2, (mm - 2) % R
                    if there(n):
                        wait(dve, s_acc, n * U + u)
                        at = acc[:, bass.ds(blks[u], 1), :].rearrange("p a d -> p (a d)")
                        nc.vector.tensor_tensor(at, at, ps_r[nm % 2][:, u * RW:(u + 1) * RW],
                                                ALU.add).then_inc(s_acc, 1)

                if there(m - 2):
                    blks = blocks_of(mybir.EngineType.DVE, m - 2)
                    dve.wait_ge(s_res, m - 2 + 1)
                add_up(0)
                n, nm = m, mm
                if there(n):
                    dve.wait_ge(s_kv[nm], (n - nm) * (16 * U // R) + 16 * U)
                    dve.wait_ge(s_q, n + 1)
                    nc.vector.tensor_tensor(prod[:, nm % 2, :].rearrange("p (u d) -> p u d", u=U),
                                            ps_q[nm % 2][:, 0:U * D].rearrange("p (u d) -> p u d", u=U),
                                            kv[:, nm, :, 0:D], ALU.mult).then_inc(s_prod, 1)
                add_up(1)
                n, nm = m - 1, (mm - 1) % R
                if there(n):
                    dve.wait_ge(s_exp, n + 1)
                    nc.vector.tensor_tensor(
                        wv[:, nm % 2, :, 0:D].rearrange("p u (h d) -> p u h d", h=HEADS),
                        kv[:, nm, :, D:2 * D].rearrange("p u (h d) -> p u h d", h=HEADS),
                        wv[:, nm % 2, :, D:RW].unsqueeze(3).to_broadcast([P, U, HEADS, DH]),
                        ALU.mult).then_inc(s_wv, 1)
                add_up(2)
                n, nm = m, mm
                if there(n):
                    dve.wait_ge(s_prod, n + 1)
                    nc.vector.tensor_reduce(score[:, nm % 2, :],
                                            prod[:, nm % 2, :].rearrange("p (h d) -> p h d", d=DH),
                                            axis=AX.X, op=ALU.add).then_inc(s_score, 1)
                add_up(3)
                n, nm = m + 2, (mm + 2) % R
                if there(n):
                    dve.wait_ge(s_locb[nm], (n - nm) * (16 // R) + 16)
                    wait(dve, s_q, n - 3)
                    wait(dve, s_ot, n - 3)
                    nc.vector.tensor_scalar(onehT[:, nm % 4, :], loc_b[:, nm, :], part1_f[:, 0:1], None,
                                            ALU.is_equal).then_inc(s_oneT, 1)
                n, nm = m, mm
                if there(n):
                    dve.wait_ge(s_score, n + 1)
                    nc.vector.tensor_scalar(clipped[:, nm % 2, :], score[:, nm % 2, :], -10.0, 10.0,
                                            ALU.max, ALU.min).then_inc(s_clip, 1)
                add_up(4)

            follow(dve, tiles, unit, {"mark": mark, "count": count, "place0": place0,
                                      "place1": place1, "own": own_position, "unpack": unpack})
            dve.wait_ge(s_acc, NT)
            link(nc.vector.tensor_scalar(den[:, :, :], acc[:, :, D:RW], 1e-8, None, ALU.add))
            nc.vector.reciprocal(den[:, :, :], den[:, :, :]).then_inc(s_den, 1)
            for i in range(NPC + 1):
                if i < NPC:
                    y = acc[:, i * PC:(i + 1) * PC, 0:D]
                    nx = PC if i < NPC - 1 else PC - 1
                    dve.wait_ge(s_xe[i % 2], 16 * (i // 2 + 1))
                    dve.wait_ge(s_div, i + 1)
                    last = nc.vector.scalar_tensor_tensor(y[:, 0:nx, :], xe[i % 2][:, 0:nx, :], 2.0, y[:, 0:nx, :],
                                                          ALU.mult, ALU.add)
                    if nx < PC:
                        last = nc.vector.scalar_tensor_tensor(y[:, nx, :], xlast[:, :], 2.0, y[:, nx, :],
                                                              ALU.mult, ALU.add)
                    link(last)
                    mu = mean[:, i % 2, :]
                    link(nc.vector.tensor_reduce(mu, y, axis=AX.X, op=ALU.add))
                    link(nc.vector.tensor_scalar(mu, mu, 1.0 / D, None, ALU.mult))
                    wait(dve, s_y, i - 1)
                    nc.vector.tensor_tensor(cent[i % 2], y, mu.unsqueeze(2).to_broadcast([P, PC, D]),
                                            ALU.subtract).then_inc(s_cent, 1)
                if i >= 1:
                    j = i - 1
                    dve.wait_ge(s_sq, j + 1)
                    link(nc.vector.tensor_reduce(var[:, j % 2, :], sq[j % 2], axis=AX.X, op=ALU.add))
                    nc.vector.tensor_scalar(var[:, j % 2, :], var[:, j % 2, :], 1.0 / D, 1e-5, ALU.mult,
                                            ALU.add).then_inc(s_var, 1)
                    dve.wait_ge(s_std, j + 1)
                    nc.vector.reciprocal(inv[:, j % 2, :], std[:, j % 2, :]).then_inc(s_inv, 1)


_INS = ['x', 'src', 'dst', 'L0_gnn_qW', 'L0_gnn_kW', 'L0_gnn_vW']
_OUTS = [((6250, 96), 'float32')]


def kernel(**inputs):
    import numpy as _np
    import concourse.bacc as _bacc
    from concourse import mybir as _mybir
    from concourse.bass_utils import run_bass_kernel_spmd as _run

    nc = _bacc.Bacc("TRN2", target_bir_lowering=False, num_devices=1)
    arrays, args = {}, []
    for name in _INS:
        a = _np.ascontiguousarray(inputs[name])
        arrays[f"in_{name}_dram"] = a
        args.append(nc.dram_tensor(f"in_{name}_dram", a.shape, _mybir.dt.from_np(a.dtype), kind="ExternalInput").ap())
    for i, (shape, dtype) in enumerate(_OUTS):
        dt = _mybir.dt.from_np(_np.dtype(dtype))
        args.append(nc.dram_tensor(f"out_{i}_dram", shape, dt, kind="ExternalOutput").ap())
    gnn(nc, *args)
    r = _run(nc, [arrays], core_ids=[0])
    got = tuple(r.results[0][f"out_{i}_dram"] for i in range(len(_OUTS)))
    return got[0]
```

```python
import concourse.bass as bass
from concourse import mybir
from contextlib import ExitStack



def gnn(nc, x, src, dst, qW, kW, vW, out):
    f32, i32, u16 = mybir.dt.float32, mybir.dt.int32, mybir.dt.uint16
    f16, bf16 = mybir.dt.float16, mybir.dt.bfloat16
    ALU = mybir.AluOpType
    ACT = mybir.ActivationFunctionType
    AX = mybir.AxisListType

    P = 128
    N, D = x.shape
    E = src.shape[0]
    HEADS = 4
    DH = D // HEADS
    NB = (N + P - 1) // P
    LASTB = N - (NB - 1) * P
    EP, EC = 125, E // 125
    assert EP * EC == E
    RW = D + HEADS
    U = 5
    R = 8
    SU = 10
    EARLY = 6
    KD = 3
    L = 7

    GC = [140, 200, 240, 270]
    G = len(GC)
    assert sum(GC) == EC and all(c % SU == 0 for c in GC)
    GT = [-(-((EP * c + NB * (P - 1)) // P) // U) * U for c in GC]
    PATTERN = [(1,) * R, (1, 1, 1, 0) * 2, (1, 1, 1, 0) * 2]
    SHARE = [(1, 2, 1, 1, 1, 2, 2, 2, 2, 2)] * (G - 1)
    C0 = [sum(GC[:g]) for g in range(G + 1)]
    V0 = [c // SU for c in C0]
    B0 = [sum(GT[:g]) // U for g in range(G + 1)]
    T0 = [b * U for b in B0]
    NT, NBT = T0[G], B0[G]
    CMAX, TMAX = max(GC), max(GT)
    assert TMAX + 1 <= 512 and P * TMAX < 1 << 16
    PC = 7
    NPC = NB // PC
    assert NPC * PC == NB
    LCH = [[(t, min(t + P, GT[g])) for t in range(0, GT[g], P)] for g in range(G)]

    PLAN = []

    def plan_iters(m, count):
        end = m + count
        looped = min(max(m, R), end)
        reps = max(0, min(end, NBT - L) - looped) // R
        PLAN.append(("iters", m, 0, [None] * (looped - m)))
        PLAN.append(("loop", looped, reps, 0, 0, (0,) * R))
        PLAN.append(("iters", looped + reps * R, 0, [None] * (end - looped - reps * R)))
        return end

    def plan_woven(m, g, pattern):
        v, end = V0[g], V0[g + 1]
        assert m >= R and sum(pattern) % 2 == 0
        PLAN.append(("iters", m, g, [v, v + 1]))
        m, v = m + 2, v + 2
        reps = (end - v) // sum(pattern)
        PLAN.append(("loop", m, reps, g, v, pattern))
        m, v = m + reps * R, v + reps * sum(pattern)
        units = []
        for k in range(2 * R):
            if v <= end:
                units.append(v if pattern[k % R] else None)
                v += pattern[k % R]
        PLAN.append(("iters", m, g, units))
        return m + len(units)

    def plan():
        RANK = ("mark", "tally0", "tally1", "tally2", "count", "place0", "place1", "place2", "own")
        ranks = [RANK[0:4], RANK[4:5], [], RANK[5:]]
        v = V0[0]
        for i in range(NPC):
            if i < len(ranks):
                for name in ranks[i]:
                    PLAN.append(("piece", name, 0))
            PLAN.append(("piece", "project", i))
            if i >= len(ranks):
                PLAN.append(("sort", 0, v, v + 2))
                v += 2
        PLAN.append(("sort", 0, v, V0[1]))
        PLAN.append(("piece", "unpack", 0))
        PLAN.append(("piece", "mark", 1))
        m = plan_iters(-L, L)
        for g in range(G - 1):
            end = B0[g + 1] - L
            pattern = PATTERN[g]
            here = len(PLAN)
            woven = plan_woven(R, g + 1, pattern) - R
            del PLAN[here:]
            spare = end - m - woven - 1
            assert spare >= 0
            share = SHARE[g]
            total = 0
            for k in range(len(RANK) + 1):
                if k and (g or k > 1):
                    PLAN.append(("piece", RANK[k - 1], g + 1))
                total += share[k]
                m = plan_iters(m, spare * total // sum(share) - spare * (total - share[k]) // sum(share))
            m = plan_woven(m, g + 1, pattern)
            m = plan_iters(m, end - m)
            PLAN.append(("piece", "unpack", g + 1))
        plan_iters(m, NBT + 2 - m)

    plan()

    kv_dram = nc.dram_tensor("kv_table", [NB * P, 2 * D], f32).ap()
    loc_dram = nc.dram_tensor("loc_rows", [NT, P], bf16).ap()

    with ExitStack() as ctx:
        def sb(name, shape, dt):
            return ctx.enter_context(nc.sbuf_tensor(name, shape, dt))

        def pb(name, shape, dt):
            return ctx.enter_context(nc.psum_tensor(name, shape, dt))

        def sem(name):
            return ctx.enter_context(nc.semaphore(name))

        iota_i = sb("iota_i", [P, TMAX + 1], i32)
        iota_f = sb("iota_f", [P, TMAX + 1], f32)
        iota_s = sb("iota_s", [P, P, SU], f16)
        iota_h = sb("iota_h", [P, GT[0] + 1], f16)
        part_i = sb("part_i", [P, 1], i32)
        part_f = sb("part_f", [P, 1], f32)
        part1_f = sb("part1_f", [P, 1], f32)
        ident_f = sb("ident_f", [P, P], f32)
        ident_bf = sb("ident_bf", [P, P], bf16)
        tri_h = sb("tri_h", [P, P], f16)
        ones_h = sb("ones_h", [P, P], f16)
        ident_h = sb("ident_h", [P, P], f16)
        w_all = sb("w_all", [D, 3 * D], f32)
        xlast = sb("xlast", [P, D], f32)
        q3 = sb("q3", [P, 3, NB, D], bf16)
        acc = sb("acc", [P, NB, RW], f32)
        src_i = sb("src_i", [EP, EC], i32)
        dst_i = sb("dst_i", [EP, EC], i32)
        tmp_i = sb("tmp_i", [EP, CMAX], i32)
        bin_u = sb("bin_u", [EP, CMAX], u16)
        pay_a = sb("pay_a", [EP, EC], f16)
        pay_b = sb("pay_b", [EP, EC], f16)
        pos_p = sb("pos_p", [EP, EC], f16)
        pos_t = sb("pos_t", [EP, EC], f32)
        steps_m = sb("steps_m", [P, NB * (CMAX + 2)], f16)
        place_m = sb("place_m", [P, NB * (CMAX + 2)], u16)
        cnt_f = sb("cnt_f", [EP, NB], f32)
        cnt = sb("cnt", [EP, NB], f16)
        step_i = sb("step_i", [EP, NB], i32)
        step_lo = sb("step_lo", [EP, NB], i32)
        need_i = sb("need_i", [P, NB], i32)
        need = sb("need", [P, NB], f32)
        tend = sb("tend", [P, NB], f32)
        tdiag = sb("tdiag", [P, NB], f32)
        tend_p = sb("tend_p", [P, 1], f32)
        after = sb("after", [P, TMAX], f16)
        firstp = sb("firstp", [P, NB], f32)
        endp = sb("endp", [P, NB], f32)
        LW = P * SU
        lhs_m = place_m[0:EP, 0:5 * LW].bitcast(f16)
        lhs_1 = lhs_m[:, 0:LW].rearrange("p (q c) -> p q c", c=SU)
        lhs_a = lhs_m[:, LW:3 * LW].rearrange("p (i q c) -> p i q c", i=2, c=SU)
        lhs_b = lhs_m[:, 3 * LW:5 * LW].rearrange("p (i q c) -> p i q c", i=2, c=SU)
        theta = steps_m[0:EP, 0:2 * SU * (TMAX + 1)].rearrange("p (i c t) -> p i c t", i=2, c=SU)
        cum_a = sb("cum_a", [P, TMAX + 1], f32)
        cum_b = sb("cum_b", [P, TMAX + 1], f32)
        dif_a = sb("dif_a", [P, TMAX], i32)
        dif_b = iota_i
        dst_s = sb("dst_s", [P, NT], i32)
        loc_s = sb("loc_s", [P, TMAX], bf16)
        loc_t = sb("loc_t", [P, 4, P], bf16)
        blk_s = sb("blk_s", [1, NT], i32)
        idx = sb("idx", [P, R, U], i32)
        kv = sb("kv", [P, R, U, 2 * D], f32)
        loc_b = sb("loc_b", [P, R, U * P], bf16)
        onehT = sb("onehT", [P, 4, U * P], bf16)
        oneh = sb("oneh", [P, 2, U, P], f32)
        prod = sb("prod", [P, 2, U * D], f32)
        score = sb("score", [P, 2, U * HEADS], f32)
        clipped = sb("clipped", [P, 2, U * HEADS], f32)
        wv = sb("wv", [P, 2, U, RW], f32)
        den = sb("den", [P, NB, HEADS], f32)
        mean = sb("mean", [P, NPC, PC], f32)
        var = sb("var", [P, NPC, PC], f32)
        std = sb("std", [P, NPC, PC], f32)
        inv = sb("inv", [P, NPC, PC], f32)

        kv_m = kv[:, :, :, :].rearrange("p r u d -> p (r u d)")
        loc_m = loc_b[:, :, :].rearrange("p r e -> p (r e)").bitcast(f32)
        CH = PC * D
        stg = kv_m[:, 0:3 * 3 * CH].rearrange("p (i b d) -> p i b d", i=3, d=3 * D)
        xc = loc_m[:, 0:2 * CH].rearrange("p (i b d) -> p i b d", i=2, d=D)
        xT = [m[0:D, a:a + PC * P].rearrange("p (b n) -> p b n", n=P)
              for m, a in ((loc_m, 2 * CH), (kv_m, 3 * 3 * CH))]

        def end_bufs(memory, first):
            return [memory[:, i * CH:(i + 1) * CH].rearrange("p (b d) -> p b d", d=D)
                    for i in range(first, first + NPC)]

        xe = end_bufs(steps_m[:, 0:2 * NPC * CH].bitcast(f32), 0)
        cent = end_bufs(place_m[:, 0:2 * NPC * CH].bitcast(f32), 0)
        yout = end_bufs(kv_m, 0)
        sq = [kv_m[:, i * CH:(i + 1) * CH].rearrange("p (b d) -> p b d", d=D) for i in (NPC, NPC + 1, NPC + 2)]

        ps_a = pb("ps_a", [P, 512], f32)
        ps_b = pb("ps_b", [P, 512], f32)
        ps_t = [pb(f"ps_t{i}", [P, 512], f32) for i in range(2)]
        ps_q = [pb(f"ps_q{i}", [P, 512], f32) for i in range(2)]
        ps_r = [pb(f"ps_r{i}", [P, 512], f32) for i in range(2)]
        ps_p = ps_r + ps_t

        s_x = [sem("s_x0"), sem("s_x1")]
        s_xe = [sem(f"s_xe{i}") for i in range(NPC)]
        s_two = sem("s_two")
        s_sum = sem("s_sum")
        s_mean = sem("s_mean")
        s_vsum = sem("s_vsum")
        s_xl = sem("s_xl")
        s_w = sem("s_w")
        s_src = sem("s_src")
        s_dst = sem("s_dst")
        s_iota = sem("s_iota")
        s_const = sem("s_const")
        s_xpad = sem("s_xpad")
        s_xt = sem("s_xt")
        s_xtc = sem("s_xtc")
        s_prj = sem("s_prj")
        s_prjc = sem("s_prjc")
        s_kvst = [sem(f"s_kvst{i}") for i in range(3)]
        s_hi = sem("s_hi")
        s_r1 = sem("s_r1")
        s_mid = sem("s_mid")
        s_lo = sem("s_lo")
        s_own = sem("s_own")
        s_mark = sem("s_mark")
        s_tally = sem("s_tally")
        s_cnt = sem("s_cnt")
        s_pre = sem("s_pre")
        s_after = sem("s_after")
        s_tab = sem("s_tab")
        s_blk = sem("s_blk")
        s_pos = sem("s_pos")
        s_lhs = sem("s_lhs")
        s_theta = sem("s_theta")
        s_bin = sem("s_bin")
        s_cum = sem("s_cum")
        s_sorted = sem("s_sorted")
        s_loc = sem("s_loc")
        s_loct = sem("s_loct")
        s_loctc = sem("s_loctc")
        s_locw = sem("s_locw")
        s_locb = [sem(f"s_locb{i}") for i in range(R)]
        s_acc0 = sem("s_acc0")
        s_idx = sem("s_idx")
        s_kv = [sem(f"s_kv{i}") for i in range(R)]
        s_oneT = sem("s_oneT")
        s_ot = sem("s_ot")
        s_one = sem("s_one")
        s_q = sem("s_q")
        s_prod = sem("s_prod")
        s_score = sem("s_score")
        s_clip = sem("s_clip")
        s_exp = sem("s_exp")
        s_wv = sem("s_wv")
        s_res = sem("s_res")
        s_acc = sem("s_acc")
        s_den = sem("s_den")
        s_div = sem("s_div")
        s_cent = sem("s_cent")
        s_sq = sem("s_sq")
        s_var = sem("s_var")
        s_std = sem("s_std")
        s_inv = sem("s_inv")
        s_y = sem("s_y")
        s_out = sem("s_out")
        s_past = sem("s_past")

        def wait(eng, s, v):
            if not (isinstance(v, int) and v <= 0):
                eng.wait_ge(s, v)

        def follow(eng, tiles, unit, pieces):
            for what in PLAN:
                if what[0] == "piece":
                    if what[1] in pieces:
                        pieces[what[1]](what[2])
                elif what[0] == "sort":
                    sort_stretch(eng, unit, *what[1:4])
                elif what[0] == "iters":
                    _, m0, g, units = what
                    for k, v in enumerate(units):
                        if v is not None and unit:
                            v -= eng is nc.tensor
                        sorts = v is not None and unit and V0[g] <= v < V0[g + 1]
                        tiles(m0 + k, (m0 + k) % R, (g, v, v % 2) if sorts else None)
                elif what[2]:
                    _, m0, reps, g, v0, pattern = what
                    v0 -= eng is nc.tensor
                    with eng.Fori(0, reps, 1) as i:
                        for k in range(R):
                            v = v0 + sum(pattern[:k])
                            sorts = pattern[k] and unit
                            tiles(i * R + (m0 + k), (m0 + k) % R,
                                  (g, i * sum(pattern) + v, v % 2) if sorts else None)

        def sort_stretch(eng, unit, g, v0, v1):
            if not unit:
                return
            a = min(v1, v0 + 2)
            b = a + max(0, v1 - 1 - a) // 2 * 2
            for v in range(v0, a):
                unit(g, v, v % 2)
            if b > a:
                with eng.Fori(a, b - 1, 2) as i:
                    for k in range(2):
                        unit(g, i + k, (a + k) % 2)
            for v in range(b, v1):
                unit(g, v, v % 2)

        def there(n):
            return not isinstance(n, int) or 0 <= n < NBT

        def blocks_of(engine, n):
            return nc.values_load_multi_w_load_instructions(
                blk_s[0:1, bass.ds(n * U, U)], engines=[engine], min_val=0, max_val=NB - 1,
                skip_runtime_bounds_check_because="clamped when the table is made")[1]

        block = ctx.enter_context(nc.Block())

        @block.sync
        def _(sp):
            def load_x(i, to, slot_sem):
                n = PC if i < NPC - 1 else PC - 1
                sp.dma_start(to[:, 0:n, :],
                             x[i * PC * P:(i * PC + n) * P, :].rearrange("(b p) d -> p b d", p=P)).then_inc(slot_sem, 16)

            sp.dma_start(src_i[:, :], src.rearrange("(p c) -> p c", c=EC)).then_inc(s_src, 16)
            load_x(0, xc[:, 0], s_x[0])
            for i, w in enumerate((qW, kW, vW)):
                sp.dma_start(w_all[:, i * D:(i + 1) * D], w).then_inc(s_w, 16)
            load_x(1, xc[:, 1], s_x[1])
            sp.dma_start(dst_i[:, :], dst.rearrange("(p c) -> p c", c=EC)).then_inc(s_dst, 16)
            sp.wait_ge(s_xpad, 1)
            sp.dma_start(xlast[0:LASTB, :], x[(NB - 1) * P:N, :]).then_inc(s_xl, 16)
            kv_rows = kv_dram.rearrange("(i b p) d -> i p b d", p=P, b=PC)
            for i in range(NPC):
                if i + 2 < NPC:
                    sp.wait_ge(s_xt, 2 * i + 2)
                    load_x(i + 2, xc[:, i % 2], s_x[i % 2])
                sp.wait_ge(s_prjc, PC * (i + 1))
                sp.dma_start(kv_rows[i], stg[:, i % 3, :, D:3 * D]).then_inc(s_kvst[i % 3], 16)

            written = 0
            for g in range(G):
                for k, (a, b) in enumerate(LCH[g]):
                    if k == 0:
                        sp.wait_ge(s_loctc, g + 1)
                    sp.dma_start(loc_dram[T0[g] + a:T0[g] + b, :], loc_t[0:b - a, k, :]).then_inc(s_locw, 16)
                    written += 16
                sp.wait_ge(s_locw, written)

                def load_rows(n, nm):
                    wait(sp, s_oneT, n - R + 1)
                    sp.dma_start(loc_b[:, nm, :],
                                 loc_dram[bass.ds(n * U, U), :].rearrange("t e -> (t e)").partition_broadcast(P)
                                 ).then_inc(s_locb[nm], 16)

                lo, hi = B0[g], B0[g + 1]
                a = max(lo, R)
                b = a + (hi - a) // R * R
                for n in range(lo, a):
                    load_rows(n, n % R)
                with sp.Fori(a, b - R + 1, R) as i:
                    for k in range(R):
                        load_rows(i + k, (a + k) % R)
                for n in range(b, hi):
                    load_rows(n, n % R)

            sp.wait_ge(s_bin, V0[G])
            for i in range(NPC):
                load_x(i, xe[i], s_xe[i])
            for i in range(NPC):
                sp.wait_ge(s_y, i + 1)
                if i < NPC - 1:
                    sp.dma_start(out[i * PC * P:(i + 1) * PC * P, :].rearrange("(b p) d -> p b d", p=P),
                                 yout[i]).then_inc(s_out, 16)
                else:
                    sp.dma_start(out[i * PC * P:(NB - 1) * P, :].rearrange("(b p) d -> p b d", p=P),
                                 yout[i][:, 0:PC - 1, :]).then_inc(s_out, 16)
                    sp.dma_start(out[(NB - 1) * P:N, :], yout[i][0:LASTB, PC - 1, :]).then_inc(s_out, 16)
            sp.wait_ge(s_out, 16 * (NPC + 1))

        @block.gpsimd
        def _(pool):
            nc.gpsimd.iota(iota_i[:, :], [[1, TMAX + 1]], base=0, channel_multiplier=0).then_inc(s_iota, 1)
            nc.gpsimd.iota(part_i[:, :], [[1, 1]], base=0, channel_multiplier=1).then_inc(s_iota, 1)
            nc.gpsimd.memset(ones_h[:, :], 1.0).then_inc(s_iota, 1)
            nc.gpsimd.memset(xlast[:, :], 0.0).then_inc(s_xpad, 1)
            nc.gpsimd.memset(acc[:, :, :], 0.0).then_inc(s_acc0, 1)
            for i in range(NPC):
                bs = slice(i * PC, (i + 1) * PC)
                qs = stg[:, i % 3, :, 0:D]
                pool.wait_ge(s_hi, i + 1)
                nc.gpsimd.tensor_tensor(qs, qs, q3[:, 0, bs, :], ALU.subtract).then_inc(s_r1, 1)
                pool.wait_ge(s_mid, i + 1)
                nc.gpsimd.tensor_tensor(q3[:, 2, bs, :], qs, q3[:, 1, bs, :], ALU.subtract).then_inc(s_lo, 1)
            for i in range(3):
                pool.wait_ge(s_kvst[i], 16 * ((NPC - i + 2) // 3))
            pool.wait_ge(s_lo, NPC)

            def tiles(m, mm, sorts):
                n, nm = m + L, (mm + L) % R
                if there(n):
                    pool.wait_ge(s_idx, n + 1)
                    pool.sem_inc(s_past, 1)
                    for u in range(U):
                        nc.gpsimd.indirect_dma_start(
                            kv[:, nm, u, :], None, kv_dram,
                            bass.IndirectOffsetOnAxis(ap=idx[:, nm, u:u + 1], axis=0)).then_inc(s_kv[nm], 16)

            follow(pool, tiles, None, {})
            pool.wait_ge(s_den, 1)
            pool.wait_ge(s_bin, V0[G])
            for i in range(NPC + 2):
                if i < NPC:
                    y = acc[:, i * PC:(i + 1) * PC, 0:D].rearrange("p b (h d) -> p b h d", h=HEADS)
                    nc.gpsimd.tensor_tensor(y, y, den[:, i * PC:(i + 1) * PC, :].unsqueeze(3)
                                            .to_broadcast([P, PC, HEADS, DH]), ALU.mult).then_inc(s_div, 1)
                if i >= 2:
                    j = i - 2
                    pool.wait_ge(s_mean, j + 1)
                    nc.gpsimd.tensor_tensor(cent[j], acc[:, j * PC:(j + 1) * PC, 0:D],
                                            mean[:, j, :].unsqueeze(2).to_broadcast([P, PC, D]),
                                            ALU.subtract).then_inc(s_cent, 1)

        @block.tensor
        def _(pe):
            def transpose_x(i):
                pe.wait_ge(s_x[i % 2], 16 * (i // 2 + 1))
                if i == 0:
                    pe.wait_ge(s_const, 1)
                if i == NPC - 1:
                    pe.wait_ge(s_xl, 16)
                for h, (a, b) in enumerate(((0, 4), (4, PC))):
                    wait(pe, s_xtc, 2 * i + h - 1)
                    for j in range(a, b):
                        xb = xlast[:, :] if i * PC + j == NB - 1 else xc[:, i % 2, j, :]
                        last = nc.tensor.transpose(ps_q[h][0:D, (j - a) * P:(j - a + 1) * P], xb, ident_f[:, :])
                    last.then_inc(s_xt, 1)

            def project(i):
                if i == 0:
                    transpose_x(0)
                if i + 1 < NPC:
                    transpose_x(i + 1)
                for j in range(PC):
                    b = i * PC + j
                    if j == 0 or j == 4:
                        pe.wait_ge(s_xtc, 2 * i + 1 + (j == 4))
                    if j == 0 and i == 0:
                        pe.wait_ge(s_w, 48)
                    wait(pe, s_prjc, b - 3)
                    nc.tensor.matmul(ps_p[b % 4][:, 0:3 * D], xT[i % 2][:, j, :], w_all[:, :],
                                     start=True, stop=True).then_inc(s_prj, 1)

            def tally(g, part):
                C = GC[g]
                steps = steps_m[0:EP, 0:NB * (C + 2)].rearrange("p (b c) -> p b c", b=NB)
                if part == 0:
                    pe.wait_ge(s_mark, g + 1)
                    wait(pe, s_loctc, g)
                for c in range(C // SU * part // 3 * SU, C // SU * (part + 1) // 3 * SU, SU):
                    last = nc.tensor.matmul(ps_a[0:EP, 0:NB * SU], ident_h[0:EP, 0:EP],
                                            steps[:, :, 2 + c:2 + c + SU], start=c == 0, stop=c == C - SU)
                if part == 2:
                    last.then_inc(s_tally, 1)

            def count(g):
                pe.wait_ge(s_cnt, g + 1)
                nc.tensor.matmul(ps_a[:, 0:NB], tri_h[0:EP, :], cnt[:, :], start=True, stop=True)
                nc.tensor.matmul(ps_a[:, 64:64 + NB], ones_h[0:EP, :], cnt[:, :],
                                 start=True, stop=True).then_inc(s_pre, 1)
                pe.wait_ge(s_after, g + 1)
                nc.tensor.matmul(ps_a[:, 0:GT[g]], ones_h[:, :], after[:, 0:GT[g]],
                                 start=True, stop=True).then_inc(s_tab, 1)

            def unit(g, v, vm):
                w = GT[g] + 1
                first = isinstance(v, int) and v == V0[g]
                last = isinstance(v, int) and v == V0[g + 1] - 1
                if first:
                    pe.wait_ge(s_blk, g + 1)
                pe.wait_ge(s_lhs, v + 1)
                wait(pe, s_theta, v + 1 - EARLY)
                for j in range(SU):
                    for ps, lhs in ((ps_a, lhs_a), (ps_b, lhs_b)):
                        mm = nc.tensor.matmul(ps[:, 0:w], lhs[:, vm, :, j], theta[:, vm, j, 0:w],
                                              start=first and j == 0, stop=last and j == SU - 1)
                mm.then_inc(s_bin, 1)

            def unpack(g):
                pe.wait_ge(s_loc, g + 1)
                for k, (a, b) in enumerate(LCH[g]):
                    last = nc.tensor.transpose(ps_a[0:b - a, k * P // 2:(k + 1) * P // 2].bitcast(bf16),
                                               loc_s[:, a:b], ident_bf[:, :])
                last.then_inc(s_loct, 1)

            def tiles(m, mm, sorts):
                n, nm = m + 1, (mm + 1) % R
                if there(n):
                    blks = blocks_of(mybir.EngineType.PE, n)
                    pe.wait_ge(s_oneT, n + 1)
                    wait(pe, s_prod, n - 1)
                    for u in range(U):
                        for i in range(3):
                            last = nc.tensor.matmul(ps_q[nm % 2][:, u * D:(u + 1) * D],
                                                    onehT[:, nm % 4, u * P:(u + 1) * P],
                                                    q3[:, i, bass.ds(blks[u], 1), :].rearrange("p a d -> p (a d)"),
                                                    start=(i == 0), stop=(i == 2))
                    last.then_inc(s_q, 1)
                n, nm = m, mm
                if there(n):
                    wait(pe, s_one, n - 1)
                    for u in range(U):
                        last = nc.tensor.transpose(ps_t[nm % 2][:, u * P // 2:(u + 1) * P // 2].bitcast(bf16),
                                                   onehT[:, nm % 4, u * P:(u + 1) * P], ident_bf[:, :])
                    last.then_inc(s_ot, 1)
                n, nm = m - 1, (mm - 1) % R
                if there(n):
                    pe.wait_ge(s_one, n + 1)
                    pe.wait_ge(s_wv, n + 1)
                    wait(pe, s_acc, U * (n - 1))
                    for u in range(U):
                        last = nc.tensor.matmul(ps_r[nm % 2][:, u * RW:(u + 1) * RW], oneh[:, nm % 2, u, :],
                                                wv[:, nm % 2, u, :], start=True, stop=True)
                    last.then_inc(s_res, 1)
                if sorts:
                    unit(*sorts)

            follow(pe, tiles, unit, {"project": project, "tally0": lambda g: tally(g, 0), "tally1": lambda g: tally(g, 1),
                                    "tally2": lambda g: tally(g, 2), "count": count, "unpack": unpack})

        @block.scalar
        def _(act):
            def copy_xt(i):
                for h, (a, b) in enumerate(((0, 4), (4, PC))):
                    act.wait_ge(s_xt, 2 * i + h + 1)
                    wait(act, s_prj, (i - 2) * PC + b)
                    nc.scalar.activation(xT[i % 2][:, a:b, :].rearrange("p b n -> p (b n)"),
                                         ps_q[h][0:D, 0:(b - a) * P], ACT.Copy).then_inc(s_xtc, 1)

            def project(i):
                if i == 0:
                    copy_xt(0)
                if i + 1 < NPC:
                    copy_xt(i + 1)
                if i >= 3:
                    act.wait_ge(s_lo, i - 2)
                    act.wait_ge(s_kvst[i % 3], 16 * (i // 3))
                for j in range(PC):
                    b = i * PC + j
                    act.wait_ge(s_prj, b + 1)
                    nc.scalar.activation(stg[:, i % 3, j, :], ps_p[b % 4][:, 0:3 * D],
                                         ACT.Copy).then_inc(s_prjc, 1)
                bs = slice(i * PC, (i + 1) * PC)
                act.wait_ge(s_prjc, PC * (i + 1))
                nc.scalar.activation(q3[:, 0, bs, :], stg[:, i % 3, :, 0:D], ACT.Copy).then_inc(s_hi, 1)
                if i:
                    split_mid(i - 1)
                if i == NPC - 1:
                    split_mid(i)

            def split_mid(i):
                act.wait_ge(s_r1, i + 1)
                nc.scalar.activation(q3[:, 1, i * PC:(i + 1) * PC, :], stg[:, i % 3, :, 0:D],
                                     ACT.Copy).then_inc(s_mid, 1)

            def unit(g, v, vm, halves=(0, 1)):
                if isinstance(v, int) and v < EARLY:
                    return
                if isinstance(v, int) and v == max(V0[g], EARLY):
                    act.wait_ge(s_pos, g + 1)
                if 0 in halves:
                    wait(act, s_bin, v - 1)
                    act.sem_inc(s_past, 1)
                w = GT[g] + 1
                for j in range(KD if g == 0 else 0, SU):
                    if j * 2 // SU in halves:
                        last = nc.scalar.activation(theta[:, vm, j, 0:w], iota_f[0:EP, 0:w], ACT.Sign, scale=-1.0,
                                                    bias=pos_t[:, bass.ds(v * SU + j, 1)])
                if 1 in halves:
                    last.then_inc(s_theta, 1)

            def unpack(g):
                w = GT[g] + 1
                act.wait_ge(s_bin, V0[g + 1])
                wait(act, s_sorted, g)
                nc.scalar.activation(cum_a[:, 0:w], ps_a[:, 0:w], ACT.Copy)
                nc.scalar.activation(cum_b[:, 0:w], ps_b[:, 0:w], ACT.Copy).then_inc(s_cum, 1)
                act.wait_ge(s_loct, g + 1)
                if g:
                    act.wait_ge(s_locw, 16 * sum(len(LCH[h]) for h in range(g)))
                for k, (a, b) in enumerate(LCH[g]):
                    last = nc.scalar.activation(loc_t[0:b - a, k, :],
                                                ps_a[0:b - a, k * P // 2:(k + 1) * P // 2].bitcast(bf16), ACT.Copy)
                last.then_inc(s_loctc, 1)
                act.wait_ge(s_sorted, g + 1)

            def tiles(m, mm, sorts):
                n, nm = m, mm
                if there(n):
                    wait(act, s_res, n - 1)
                    act.wait_ge(s_ot, n + 1)
                    nc.scalar.activation(oneh[:, nm % 2, :, :].rearrange("p u n -> p (u n)"),
                                         ps_t[nm % 2][:, 0:U * P // 2].bitcast(bf16), ACT.Copy).then_inc(s_one, 1)
                if sorts:
                    unit(*sorts, halves=(0,))
                if there(n):
                    act.wait_ge(s_clip, n + 1)
                    nc.scalar.activation(wv[:, nm % 2, :, D:RW],
                                         clipped[:, nm % 2, :].rearrange("p (u h) -> p u h", h=HEADS),
                                         ACT.Exp).then_inc(s_exp, 1)
                n, nm = m + L, (mm + L) % R
                if there(n):
                    stage(n, nm)
                if sorts:
                    unit(*sorts, halves=(1,))

            def stage(n, nm):
                wait(act, s_wv, n - R + 1)
                act.sem_inc(s_past, 1)
                nc.scalar.activation(idx[:, nm, :], dst_s[:, bass.ds(n * U, U)], ACT.Copy).then_inc(s_idx, 1)

            follow(act, tiles, unit, {"project": project, "unpack": unpack})
            act.wait_ge(s_wv, NBT)
            for i in range(NPC + 2):
                if i < NPC:
                    act.wait_ge(s_cent, i + 1)
                    wait(act, s_vsum, i - 2)
                    nc.scalar.activation(sq[i % 3], cent[i], ACT.Square).then_inc(s_sq, 1)
                if 1 <= i <= NPC:
                    act.wait_ge(s_var, i)
                    nc.scalar.activation(std[:, i - 1, :], var[:, i - 1, :], ACT.Sqrt).then_inc(s_std, 1)
                if i >= 2:
                    j = i - 2
                    act.wait_ge(s_inv, j + 1)
                    for b in range(PC):
                        last = nc.scalar.activation(yout[j][:, b, :], cent[j][:, b, :], ACT.Copy,
                                                    scale=inv[:, j, b:b + 1])
                    last.then_inc(s_y, 1)

        @block.vector
        def _(dve):
            own = [0]

            def link(ins):
                own[0] += 1
                ins.then_inc(s_own, 1)
                dve.wait_ge(s_own, own[0])

            dve.wait_ge(s_iota, 3)
            nc.vector.tensor_copy(iota_f[:, :], iota_i[:, :])
            nc.vector.tensor_copy(iota_h[:, :], iota_i[:, 0:GT[0] + 1])
            link(nc.vector.tensor_copy(part_f[:, :], part_i[:, :]))
            nc.vector.tensor_scalar(part1_f[:, :], part_f[:, :], 1.0, None, ALU.add)
            nc.vector.tensor_scalar(ident_bf[:, :], iota_f[:, 0:P], part_f[:, 0:1], None, ALU.is_equal)
            nc.vector.tensor_scalar(ident_h[:, :], iota_f[:, 0:P], part_f[:, 0:1], None, ALU.is_equal)
            nc.vector.tensor_scalar(tri_h[:, :], iota_f[:, 0:P], part_f[:, 0:1], None, ALU.is_gt)
            nc.vector.tensor_scalar(ident_f[:, :], iota_f[:, 0:P], part_f[:, 0:1], None,
                                    ALU.is_equal).then_inc(s_const, 1)
            dve.wait_ge(s_const, 1)

            def group_views(g):
                C = GC[g]
                return (C, steps_m[0:EP, 0:NB * (C + 2)].rearrange("p (b c) -> p b c", b=NB),
                        place_m[0:EP, 0:NB * (C + 2)].rearrange("p (b c) -> p b c", b=NB))

            def mark(g):
                C, c0, c1 = GC[g], C0[g], C0[g + 1]
                s, d, t = src_i[:, c0:c1], dst_i[:, c0:c1], tmp_i[:, 0:C]
                _, steps, _ = group_views(g)
                if g == 0:
                    dve.wait_ge(s_src, 16)
                link(nc.vector.tensor_scalar(t, s, 7, None, ALU.logical_shift_right))
                link(nc.vector.tensor_copy(bin_u[:, 0:C], t))
                for b in range(NB):
                    last = nc.vector.tensor_scalar(steps[:, b, 2:C + 2], bin_u[:, 0:C], float(b), None, ALU.is_equal)
                last.then_inc(s_mark, 1)
                if g == 0:
                    dve.wait_ge(s_dst, 16)
                link(nc.vector.tensor_scalar(s, s, P - 1, 3, ALU.bitwise_and, ALU.logical_shift_left))
                link(nc.vector.tensor_scalar(t, d, 10, None, ALU.logical_shift_right))
                link(nc.vector.scalar_tensor_tensor(pay_a[:, c0:c1], s, 8.0, t, ALU.add, ALU.add))
                link(nc.vector.tensor_scalar(t, d, 1023, None, ALU.bitwise_and))
                link(nc.vector.tensor_copy(pay_b[:, c0:c1], t))

            def count(g):
                C, steps, _ = group_views(g)
                dve.wait_ge(s_tally, g + 1)
                link(nc.vector.tensor_reduce(cnt_f[:, :], ps_a[0:EP, 0:NB * SU].rearrange("p (b c) -> p b c", c=SU),
                                             axis=AX.X, op=ALU.add))
                nc.vector.tensor_copy(cnt[:, :], cnt_f[:, :]).then_inc(s_cnt, 1)
                dve.wait_ge(s_pre, g + 1)
                link(nc.vector.tensor_scalar(need_i[:, :], ps_a[:, 64:64 + NB], float(P - 1), None, ALU.add))
                link(nc.vector.tensor_scalar(need_i[:, :], need_i[:, :], 7, None, ALU.logical_shift_right))
                link(nc.vector.tensor_copy(need[:, :], need_i[:, :]))
                link(nc.vector.tensor_tensor_scan(tend[:, :], need[:, :], need[:, :], 0.0, ALU.add, ALU.max))
                link(nc.vector.tensor_tensor(tdiag[:, :], tend[:, :], ident_f[:, 0:NB], ALU.mult))
                link(nc.vector.tensor_reduce(tend_p[:, :], tdiag[:, :], axis=AX.X, op=ALU.add))
                link(nc.vector.tensor_tensor(need[:, :], tend[:, :], need[:, :], ALU.subtract))
                link(nc.vector.scalar_tensor_tensor(firstp[:, :], need[:, :], float(P), ps_a[:, 0:NB],
                                                    ALU.mult, ALU.add))
                nc.vector.tensor_scalar(after[:, 0:GT[g]], iota_f[:, 0:GT[g]], tend_p[:, 0:1], None,
                                        ALU.is_ge).then_inc(s_after, 1)
                link(nc.vector.tensor_tensor(endp[0:EP, :], firstp[0:EP, :], cnt_f[:, :], ALU.add))
                nc.vector.tensor_copy(step_i[:, 0:1], firstp[0:EP, 0:1])
                link(nc.vector.tensor_tensor(step_i[:, 1:NB], firstp[0:EP, 1:NB], endp[0:EP, 0:NB - 1],
                                             ALU.subtract))
                link(nc.vector.tensor_scalar(step_lo[:, :], step_i[:, :], 1023, None, ALU.bitwise_and))
                nc.vector.tensor_copy(steps[:, :, 1], step_lo[:, :])
                link(nc.vector.tensor_tensor(steps[:, :, 0], step_i[:, :], step_lo[:, :], ALU.subtract))
                dve.wait_ge(s_tab, g + 1)
                nc.vector.tensor_scalar(blk_s[0:1, T0[g]:T0[g + 1]], ps_a[0:1, 0:GT[g]], float(NB - P),
                                        float(NB - 1), ALU.add, ALU.min).then_inc(s_blk, 1)

            def place(g, b0, b1):
                C, steps, pl = group_views(g)
                a, b = b0 * (C + 2), b1 * (C + 2)
                link(nc.vector.tensor_tensor_scan(place_m[0:EP, a:b], steps_m[0:EP, a:b], steps_m[0:EP, a:b],
                                                  0.0 if b0 == 0 else endp[0:EP, b0 - 1:b0], ALU.add, ALU.max))
                link(nc.vector.tensor_tensor(pl[:, b0:b1, 2:C + 2], pl[:, b0:b1, 2:C + 2],
                                             steps[:, b0:b1, 2:C + 2], ALU.mult))

            def own_position(g):
                C, _, pl = group_views(g)
                c0, c1 = C0[g], C0[g + 1]
                n = NB
                while n > 1:
                    h = n // 2
                    link(nc.vector.tensor_tensor(pl[:, 0:h, 2:C + 2], pl[:, 0:h, 2:C + 2],
                                                 pl[:, n - h:n, 2:C + 2], ALU.add))
                    n -= h
                t, s = tmp_i[:, 0:C], src_i[:, c0:c1]
                link(nc.vector.tensor_scalar(t, pl[:, 0, 2:C + 2], -1.0, None, ALU.add))
                link(nc.vector.tensor_scalar(s, t, P - 1, None, ALU.bitwise_and))
                link(nc.vector.tensor_copy(pos_p[:, c0:c1], s))
                link(nc.vector.tensor_scalar(t, t, 7, None, ALU.logical_shift_right))
                nc.vector.tensor_scalar(pos_t[:, c0:c1], t, 0.5, None, ALU.add).then_inc(s_pos, 1)
                dve.wait_ge(s_pos, g + 1)
                if g == 0:
                    link(nc.vector.tensor_copy(iota_s[:, :, :],
                                               iota_f[:, 0:P].unsqueeze(2).to_broadcast([P, P, SU])))

            def unit(g, v, vm, between=lambda i: None):
                wait(dve, s_bin, v - 1)
                cols = bass.ds(v * SU, SU)

                def spread(a):
                    return a[:, cols].unsqueeze(1).to_broadcast([EP, P, SU])

                if g == 0:
                    for j in range(SU if isinstance(v, int) and v < EARLY else KD):
                        nc.vector.tensor_scalar(theta[:, vm, j, 0:GT[g] + 1], iota_h[0:EP, 0:GT[g] + 1],
                                                pos_t[:, bass.ds(v * SU + j, 1)], 2.0, ALU.is_le, ALU.mult)
                wait(dve, s_lhs, v)
                nc.vector.tensor_tensor(lhs_1[:, :, :], iota_s[0:EP, :, :], spread(pos_p),
                                        ALU.is_equal).then_inc(s_one_lhs, 1)
                between(0)
                dve.wait_ge(s_one_lhs, v + 1)
                nc.vector.tensor_tensor(lhs_a[:, vm, :, :], lhs_1[:, :, :], spread(pay_a), ALU.mult)
                between(1)
                nc.vector.tensor_tensor(lhs_b[:, vm, :, :], lhs_1[:, :, :], spread(pay_b),
                                        ALU.mult).then_inc(s_lhs, 1)

            s_one_lhs = sem("s_one_lhs")

            def unpack(g):
                T, t0 = GT[g], T0[g]
                dve.wait_ge(s_cum, g + 1)
                link(nc.vector.tensor_tensor(dif_a[:, 0:T], cum_a[:, 0:T], cum_a[:, 1:T + 1], ALU.subtract))
                link(nc.vector.tensor_scalar(dif_b[:, 0:T], dif_a[:, 0:T], 4, None, ALU.logical_shift_right))
                link(nc.vector.tensor_copy(loc_s[:, 0:T], dif_b[:, 0:T]))
                link(nc.vector.tensor_scalar(dif_a[:, 0:T], dif_a[:, 0:T], 14, 9, ALU.bitwise_and,
                                             ALU.logical_shift_left))
                nc.vector.tensor_tensor(dif_b[:, 0:T], cum_b[:, 0:T], cum_b[:, 1:T + 1],
                                        ALU.subtract).then_inc(s_loc, 1)
                dve.wait_ge(s_loc, g + 1)
                link(nc.vector.tensor_scalar(dif_b[:, 0:T], dif_b[:, 0:T], 1, None, ALU.logical_shift_right))
                nc.vector.tensor_tensor(dst_s[:, t0:t0 + T], dif_a[:, 0:T], dif_b[:, 0:T],
                                        ALU.bitwise_or).then_inc(s_sorted, 1)
                dve.wait_ge(s_sorted, g + 1)
                if g == 0:
                    dve.wait_ge(s_acc0, 1)

            def tiles(m, mm, sorts):
                def add_up(u):
                    n, nm = m - 2, (mm - 2) % R
                    if there(n):
                        wait(dve, s_acc, n * U + u)
                        at = acc[:, bass.ds(blks[u], 1), :].rearrange("p a d -> p (a d)")
                        nc.vector.tensor_tensor(at, at, ps_r[nm % 2][:, u * RW:(u + 1) * RW],
                                                ALU.add).then_inc(s_acc, 1)

                n, nm = m, mm
                if there(n):
                    dve.wait_ge(s_kv[nm], (n - nm) * (16 * U // R) + 16 * U)
                    dve.wait_ge(s_q, n + 1)
                    nc.vector.tensor_tensor(prod[:, nm % 2, :].rearrange("p (u d) -> p u d", u=U),
                                            ps_q[nm % 2][:, 0:U * D].rearrange("p (u d) -> p u d", u=U),
                                            kv[:, nm, :, 0:D], ALU.mult).then_inc(s_prod, 1)
                n, nm = m - 1, (mm - 1) % R
                if there(n):
                    dve.wait_ge(s_exp, n + 1)
                    nc.vector.tensor_tensor(
                        wv[:, nm % 2, :, 0:D].rearrange("p u (h d) -> p u h d", h=HEADS),
                        kv[:, nm, :, D:2 * D].rearrange("p u (h d) -> p u h d", h=HEADS),
                        wv[:, nm % 2, :, D:RW].unsqueeze(3).to_broadcast([P, U, HEADS, DH]),
                        ALU.mult).then_inc(s_wv, 1)
                if there(m - 2):
                    blks = blocks_of(mybir.EngineType.DVE, m - 2)
                    dve.wait_ge(s_res, m - 2 + 1)
                add_up(0)
                n, nm = m, mm
                if there(n):
                    dve.wait_ge(s_prod, n + 1)
                    nc.vector.tensor_reduce(score[:, nm % 2, :],
                                            prod[:, nm % 2, :].rearrange("p (h d) -> p h d", d=DH),
                                            axis=AX.X, op=ALU.add).then_inc(s_score, 1)
                add_up(1)
                n, nm = m + 2, (mm + 2) % R
                if there(n):
                    dve.wait_ge(s_locb[nm], (n - nm) * (16 // R) + 16)
                    wait(dve, s_q, n - 3)
                    wait(dve, s_ot, n - 3)
                    nc.vector.tensor_scalar(onehT[:, nm % 4, :], loc_b[:, nm, :], part1_f[:, 0:1], None,
                                            ALU.is_equal).then_inc(s_oneT, 1)
                n, nm = m, mm
                if there(n):
                    dve.wait_ge(s_score, n + 1)
                    nc.vector.tensor_scalar(clipped[:, nm % 2, :], score[:, nm % 2, :], -10.0, 10.0,
                                            ALU.max, ALU.min).then_inc(s_clip, 1)
                add_up(2)
                if sorts:
                    unit(*sorts, between=lambda i: add_up(3 + i))
                else:
                    add_up(3)
                    add_up(4)

            follow(dve, tiles, unit, {"mark": mark, "count": count, **{f"place{i}": lambda g, i=i: place(g, NB * i // 3, NB * (i + 1) // 3)
                                                    for i in range(3)},
                                      "own": own_position, "unpack": unpack})
            dve.wait_ge(s_acc, NT)
            link(nc.vector.tensor_scalar(den[:, :, :], acc[:, :, D:RW], 1e-8, None, ALU.add))
            nc.vector.reciprocal(den[:, :, :], den[:, :, :]).then_inc(s_den, 1)
            for i in range(NPC + 4):
                if i < NPC:
                    y = acc[:, i * PC:(i + 1) * PC, 0:D]
                    nx = PC if i < NPC - 1 else PC - 1
                    dve.wait_ge(s_xe[i], 16)
                    dve.wait_ge(s_div, i + 1)
                    last = nc.vector.scalar_tensor_tensor(y[:, 0:nx, :], xe[i][:, 0:nx, :], 2.0, y[:, 0:nx, :],
                                                          ALU.mult, ALU.add)
                    if nx < PC:
                        last = nc.vector.scalar_tensor_tensor(y[:, nx, :], xlast[:, :], 2.0, y[:, nx, :],
                                                              ALU.mult, ALU.add)
                    last.then_inc(s_two, 1)
                j = i - 3
                if 0 <= j < NPC:
                    dve.wait_ge(s_sq, j + 1)
                    nc.vector.tensor_reduce(var[:, j, :], sq[j % 3], axis=AX.X, op=ALU.add).then_inc(s_vsum, 1)
                if i < NPC:
                    dve.wait_ge(s_two, i + 1)
                    nc.vector.tensor_reduce(mean[:, i, :], y, axis=AX.X, op=ALU.add).then_inc(s_sum, 1)
                if 0 <= j < NPC:
                    dve.wait_ge(s_vsum, j + 1)
                    nc.vector.tensor_scalar(var[:, j, :], var[:, j, :], 1.0 / D, 1e-5, ALU.mult,
                                            ALU.add).then_inc(s_var, 1)
                if i < NPC:
                    dve.wait_ge(s_sum, i + 1)
                    nc.vector.tensor_scalar(mean[:, i, :], mean[:, i, :], 1.0 / D, None, ALU.mult).then_inc(s_mean, 1)
                if i >= 4:
                    dve.wait_ge(s_std, i - 3)
                    nc.vector.reciprocal(inv[:, i - 4, :], std[:, i - 4, :]).then_inc(s_inv, 1)


_INS = ['x', 'src', 'dst', 'L0_gnn_qW', 'L0_gnn_kW', 'L0_gnn_vW']
_OUTS = [((6250, 96), 'float32')]


def kernel(**inputs):
    import numpy as _np
    import concourse.bacc as _bacc
    from concourse import mybir as _mybir
    from concourse.bass_utils import run_bass_kernel_spmd as _run

    nc = _bacc.Bacc("TRN2", target_bir_lowering=False, num_devices=1)
    arrays, args = {}, []
    for name in _INS:
        a = _np.ascontiguousarray(inputs[name])
        arrays[f"in_{name}_dram"] = a
        args.append(nc.dram_tensor(f"in_{name}_dram", a.shape, _mybir.dt.from_np(a.dtype), kind="ExternalInput").ap())
    for i, (shape, dtype) in enumerate(_OUTS):
        dt = _mybir.dt.from_np(_np.dtype(dtype))
        args.append(nc.dram_tensor(f"out_{i}_dram", shape, dt, kind="ExternalOutput").ap())
    gnn(nc, *args)
    r = _run(nc, [arrays], core_ids=[0])
    got = tuple(r.results[0][f"out_{i}_dram"] for i in range(len(_OUTS)))
    return got[0]
```
